# Optimizing a Trainium2 kernel written in Bass

```python
import numpy as np
import jax
import jax.numpy as jnp

def _softmax(x, axis=-1):
    return jax.nn.softmax(x, axis=axis)

def _gelu(x):
    return jax.nn.gelu(x, approximate=True)

def _silu(x):
    return jax.nn.silu(x)

def _sigmoid(x):
    return jax.nn.sigmoid(x)

def _layernorm(x, axis=-1, eps=1e-05):
    m = jnp.mean(x, axis=axis, keepdims=True)
    v = jnp.var(x, axis=axis, keepdims=True)
    return (x - m) / jnp.sqrt(v + eps)

def _scatter_add(tgt, idx, src, axis=0):
    return tgt.at[idx].add(src)

def _segment_sum(src, seg, n):
    return jax.ops.segment_sum(src, seg, n)
kernel_name = 'mk_prb_d1_jaxref_r8_f14b0e'

def setup_inputs(seed: int=0):
    np.random.seed(seed)
    _w = jnp.asarray

    def _L0_attn_setup():
        import jax, jax.numpy as jnp
        import numpy as np
        D_MODEL = 128
        N_LAYERS = 2
        N_HEADS = 16
        HEAD_DIM = D_MODEL // N_HEADS
        D_FFN = 4 * D_MODEL
        B, L = (4, 128)

        def layer_norm(x, g, b, eps=1e-05):
            mu = jnp.mean(x, axis=-1, keepdims=True)
            var = jnp.var(x, axis=-1, keepdims=True)
            return (x - mu) * jax.lax.rsqrt(var + eps) * g + b

        def make_decay(length):
            gamma = 1.0 - 2.0 ** (-5.0 - jnp.arange(N_HEADS, dtype=jnp.float32))
            n = jnp.arange(length, dtype=jnp.float32)[:, None]
            m = jnp.arange(length, dtype=jnp.float32)[None, :]
            diff = n - m
            pow_ = gamma[:, None, None] ** diff[None]
            return jnp.where(diff[None] >= 0, pow_, 0.0)

        def _forward(x, proj_w, proj_b, reto_w, reto_b, ln1_g, ln1_b, ln2_g, ln2_b, ffn1_w, ffn1_b, ffn2_w, ffn2_b, lnf_g, lnf_b):
            Bx, Lx, _ = x.shape
            D = make_decay(Lx)
            for i in range(N_LAYERS):
                ln_x = layer_norm(x, ln1_g[i], ln1_b[i])
                p = ln_x @ proj_w[i] + proj_b[i]
                q, k, v, xo = jnp.split(p, 4, axis=-1)
                q = q.reshape(Bx, Lx, N_HEADS, HEAD_DIM).transpose(0, 2, 1, 3)
                k = k.reshape(Bx, Lx, N_HEADS, HEAD_DIM).transpose(0, 2, 1, 3)
                v = v.reshape(Bx, Lx, N_HEADS, HEAD_DIM).transpose(0, 2, 1, 3)
                scores = jnp.einsum('bhld,bhmd->bhlm', q, k) * D[None]
                ret = jnp.einsum('bhlm,bhmd->bhld', scores, v)
                ret = ret.transpose(0, 2, 1, 3).reshape(Bx, Lx, D_MODEL)
                ret = ret * jax.nn.silu(xo)
                ret = ret @ reto_w[i] + reto_b[i]
                x = x + ret
                h = layer_norm(x, ln2_g[i], ln2_b[i])
                h = jax.nn.gelu(h @ ffn1_w[i] + ffn1_b[i], approximate=False) @ ffn2_w[i] + ffn2_b[i]
                x = x + h
            return layer_norm(x, lnf_g, lnf_b)
        key = jax.random.key(seed)
        ks = jax.random.split(key, 16)
        s = 0.02
        inp = {'x': jax.random.normal(ks[0], (B, L, D_MODEL), jnp.float32), 'proj_w': jax.random.normal(ks[1], (N_LAYERS, D_MODEL, 4 * D_MODEL), jnp.float32) * s, 'proj_b': jnp.zeros((N_LAYERS, 4 * D_MODEL), jnp.float32), 'reto_w': jax.random.normal(ks[2], (N_LAYERS, D_MODEL, D_MODEL), jnp.float32) * s, 'reto_b': jnp.zeros((N_LAYERS, D_MODEL), jnp.float32), 'ln1_g': jnp.ones((N_LAYERS, D_MODEL), jnp.float32), 'ln1_b': jnp.zeros((N_LAYERS, D_MODEL), jnp.float32), 'ln2_g': jnp.ones((N_LAYERS, D_MODEL), jnp.float32), 'ln2_b': jnp.zeros((N_LAYERS, D_MODEL), jnp.float32), 'ffn1_w': jax.random.normal(ks[3], (N_LAYERS, D_MODEL, D_FFN), jnp.float32) * s, 'ffn1_b': jnp.zeros((N_LAYERS, D_FFN), jnp.float32), 'ffn2_w': jax.random.normal(ks[4], (N_LAYERS, D_FFN, D_MODEL), jnp.float32) * s, 'ffn2_b': jnp.zeros((N_LAYERS, D_MODEL), jnp.float32), 'lnf_g': jnp.ones((D_MODEL,), jnp.float32), 'lnf_b': jnp.zeros((D_MODEL,), jnp.float32)}
        return inp
    _L0_attn_in = _L0_attn_setup()

    def _L0_ffn_setup():
        import jax, jax.numpy as jnp
        import numpy as np
        D = 128
        H = 256
        E = 8
        TOP_K = 2
        N_SHARED = 2
        B, S = (2, 512)

        def _moe_forward(x, gate_w, gate_b, w1, b1, w2, b2, w3, b3, sw1, sb1, sw2, sb2, sw3, sb3):
            bsz, seq_len, d = x.shape
            xf = x.reshape(-1, d)
            N = xf.shape[0]
            logits = xf @ gate_w.T + gate_b
            scores = jax.nn.softmax(logits, axis=-1)
            topk_w, topk_idx = jax.lax.top_k(scores, TOP_K)
            topk_w = topk_w / (topk_w.sum(-1, keepdims=True) + 1e-20)
            cw = jnp.zeros((N, E), xf.dtype).at[jnp.arange(N)[:, None], topk_idx].add(topk_w)
            y = jnp.zeros_like(xf)
            for e in range(E):
                h = jax.nn.silu(xf @ w1[e].T + b1[e]) * (xf @ w3[e].T + b3[e])
                y = y + cw[:, e:e + 1] * (h @ w2[e].T + b2[e])
            hs = jax.nn.silu(xf @ sw1.T + sb1) * (xf @ sw3.T + sb3)
            ys = hs @ sw2.T + sb2
            return (y + ys).reshape(bsz, seq_len, d)
        key = jax.random.key(seed)
        ks = jax.random.split(key, 16)
        sc = 0.02
        HS = N_SHARED * H
        return {'x': jax.random.normal(ks[0], (B, S, D), jnp.float32), 'gate_w': jax.random.normal(ks[1], (E, D), jnp.float32) * sc, 'gate_b': jax.random.normal(ks[2], (E,), jnp.float32) * sc, 'w1': jax.random.normal(ks[3], (E, H, D), jnp.float32) * sc, 'b1': jax.random.normal(ks[4], (E, H), jnp.float32) * sc, 'w2': jax.random.normal(ks[5], (E, D, H), jnp.float32) * sc, 'b2': jax.random.normal(ks[6], (E, D), jnp.float32) * sc, 'w3': jax.random.normal(ks[7], (E, H, D), jnp.float32) * sc, 'b3': jax.random.normal(ks[8], (E, H), jnp.float32) * sc, 'sw1': jax.random.normal(ks[9], (HS, D), jnp.float32) * sc, 'sb1': jax.random.normal(ks[10], (HS,), jnp.float32) * sc, 'sw2': jax.random.normal(ks[11], (D, HS), jnp.float32) * sc, 'sb2': jax.random.normal(ks[12], (D,), jnp.float32) * sc, 'sw3': jax.random.normal(ks[13], (HS, D), jnp.float32) * sc, 'sb3': jax.random.normal(ks[14], (HS,), jnp.float32) * sc}
    _L0_ffn_in = _L0_ffn_setup()
    _d = {'L0_attn_x': _L0_attn_in['x'], 'L0_attn_proj_w': _L0_attn_in['proj_w'], 'L0_attn_proj_b': _L0_attn_in['proj_b'], 'L0_attn_reto_w': _L0_attn_in['reto_w'], 'L0_attn_reto_b': _L0_attn_in['reto_b'], 'L0_attn_ln1_g': _L0_attn_in['ln1_g'], 'L0_attn_ln1_b': _L0_attn_in['ln1_b'], 'L0_attn_ln2_g': _L0_attn_in['ln2_g'], 'L0_attn_ln2_b': _L0_attn_in['ln2_b'], 'L0_attn_ffn1_w': _L0_attn_in['ffn1_w'], 'L0_attn_ffn1_b': _L0_attn_in['ffn1_b'], 'L0_attn_ffn2_w': _L0_attn_in['ffn2_w'], 'L0_attn_ffn2_b': _L0_attn_in['ffn2_b'], 'L0_attn_lnf_g': _L0_attn_in['lnf_g'], 'L0_attn_lnf_b': _L0_attn_in['lnf_b'], 'L0_ffn_gate_w': _L0_ffn_in['gate_w'], 'L0_ffn_gate_b': _L0_ffn_in['gate_b'], 'L0_ffn_w1': _L0_ffn_in['w1'], 'L0_ffn_b1': _L0_ffn_in['b1'], 'L0_ffn_w2': _L0_ffn_in['w2'], 'L0_ffn_b2': _L0_ffn_in['b2'], 'L0_ffn_w3': _L0_ffn_in['w3'], 'L0_ffn_b3': _L0_ffn_in['b3'], 'L0_ffn_sw1': _L0_ffn_in['sw1'], 'L0_ffn_sb1': _L0_ffn_in['sb1'], 'L0_ffn_sw2': _L0_ffn_in['sw2'], 'L0_ffn_sb2': _L0_ffn_in['sb2'], 'L0_ffn_sw3': _L0_ffn_in['sw3'], 'L0_ffn_sb3': _L0_ffn_in['sb3']}
    _x0 = _d['L0_attn_x']
    _d['L0_attn_x'] = jax.random.normal(jax.random.fold_in(jax.random.key(seed), 1), (1, 2048, 128), dtype=_x0.dtype)
    del _x0
    return _d

def reference(L0_attn_x, L0_attn_proj_w, L0_attn_proj_b, L0_attn_reto_w, L0_attn_reto_b, L0_attn_ln1_g, L0_attn_ln1_b, L0_attn_ln2_g, L0_attn_ln2_b, L0_attn_ffn1_w, L0_attn_ffn1_b, L0_attn_ffn2_w, L0_attn_ffn2_b, L0_attn_lnf_g, L0_attn_lnf_b, L0_ffn_gate_w, L0_ffn_gate_b, L0_ffn_w1, L0_ffn_b1, L0_ffn_w2, L0_ffn_b2, L0_ffn_w3, L0_ffn_b3, L0_ffn_sw1, L0_ffn_sb1, L0_ffn_sw2, L0_ffn_sb2, L0_ffn_sw3, L0_ffn_sb3):

    def _L0_attn_ref(x, proj_w, proj_b, reto_w, reto_b, ln1_g, ln1_b, ln2_g, ln2_b, ffn1_w, ffn1_b, ffn2_w, ffn2_b, lnf_g, lnf_b):
        import jax, jax.numpy as jnp
        import numpy as np
        D_MODEL = 128
        N_LAYERS = 2
        N_HEADS = 16
        HEAD_DIM = D_MODEL // N_HEADS
        D_FFN = 4 * D_MODEL
        B, L = (4, 128)

        def layer_norm(x, g, b, eps=1e-05):
            mu = jnp.mean(x, axis=-1, keepdims=True)
            var = jnp.var(x, axis=-1, keepdims=True)
            return (x - mu) * jax.lax.rsqrt(var + eps) * g + b

        def make_decay(length):
            gamma = 1.0 - 2.0 ** (-5.0 - jnp.arange(N_HEADS, dtype=jnp.float32))
            n = jnp.arange(length, dtype=jnp.float32)[:, None]
            m = jnp.arange(length, dtype=jnp.float32)[None, :]
            diff = n - m
            pow_ = gamma[:, None, None] ** diff[None]
            return jnp.where(diff[None] >= 0, pow_, 0.0)

        def _forward(x, proj_w, proj_b, reto_w, reto_b, ln1_g, ln1_b, ln2_g, ln2_b, ffn1_w, ffn1_b, ffn2_w, ffn2_b, lnf_g, lnf_b):
            Bx, Lx, _ = x.shape
            D = make_decay(Lx)
            for i in range(N_LAYERS):
                ln_x = layer_norm(x, ln1_g[i], ln1_b[i])
                p = ln_x @ proj_w[i] + proj_b[i]
                q, k, v, xo = jnp.split(p, 4, axis=-1)
                q = q.reshape(Bx, Lx, N_HEADS, HEAD_DIM).transpose(0, 2, 1, 3)
                k = k.reshape(Bx, Lx, N_HEADS, HEAD_DIM).transpose(0, 2, 1, 3)
                v = v.reshape(Bx, Lx, N_HEADS, HEAD_DIM).transpose(0, 2, 1, 3)
                scores = jnp.einsum('bhld,bhmd->bhlm', q, k) * D[None]
                ret = jnp.einsum('bhlm,bhmd->bhld', scores, v)
                ret = ret.transpose(0, 2, 1, 3).reshape(Bx, Lx, D_MODEL)
                ret = ret * jax.nn.silu(xo)
                ret = ret @ reto_w[i] + reto_b[i]
                x = x + ret
                h = layer_norm(x, ln2_g[i], ln2_b[i])
                h = jax.nn.gelu(h @ ffn1_w[i] + ffn1_b[i], approximate=False) @ ffn2_w[i] + ffn2_b[i]
                x = x + h
            return layer_norm(x, lnf_g, lnf_b)
        return _forward(x, proj_w, proj_b, reto_w, reto_b, ln1_g, ln1_b, ln2_g, ln2_b, ffn1_w, ffn1_b, ffn2_w, ffn2_b, lnf_g, lnf_b)

    def _L0_ffn_ref(x, gate_w, gate_b, w1, b1, w2, b2, w3, b3, sw1, sb1, sw2, sb2, sw3, sb3):
        import jax, jax.numpy as jnp
        import numpy as np
        D = 128
        H = 256
        E = 8
        TOP_K = 2
        N_SHARED = 2
        B, S = (2, 512)

        def _moe_forward(x, gate_w, gate_b, w1, b1, w2, b2, w3, b3, sw1, sb1, sw2, sb2, sw3, sb3):
            bsz, seq_len, d = x.shape
            xf = x.reshape(-1, d)
            N = xf.shape[0]
            logits = xf @ gate_w.T + gate_b
            scores = jax.nn.softmax(logits, axis=-1)
            topk_w, topk_idx = jax.lax.top_k(scores, TOP_K)
            topk_w = topk_w / (topk_w.sum(-1, keepdims=True) + 1e-20)
            cw = jnp.zeros((N, E), xf.dtype).at[jnp.arange(N)[:, None], topk_idx].add(topk_w)
            y = jnp.zeros_like(xf)
            for e in range(E):
                h = jax.nn.silu(xf @ w1[e].T + b1[e]) * (xf @ w3[e].T + b3[e])
                y = y + cw[:, e:e + 1] * (h @ w2[e].T + b2[e])
            hs = jax.nn.silu(xf @ sw1.T + sb1) * (xf @ sw3.T + sb3)
            ys = hs @ sw2.T + sb2
            return (y + ys).reshape(bsz, seq_len, d)
        return _moe_forward(x, gate_w, gate_b, w1, b1, w2, b2, w3, b3, sw1, sb1, sw2, sb2, sw3, sb3)
    x = L0_attn_x
    xn = _layernorm(x, axis=-1)
    x = x + _L0_attn_ref(xn, L0_attn_proj_w, L0_attn_proj_b, L0_attn_reto_w, L0_attn_reto_b, L0_attn_ln1_g, L0_attn_ln1_b, L0_attn_ln2_g, L0_attn_ln2_b, L0_attn_ffn1_w, L0_attn_ffn1_b, L0_attn_ffn2_w, L0_attn_ffn2_b, L0_attn_lnf_g, L0_attn_lnf_b) + _L0_ffn_ref(xn, L0_ffn_gate_w, L0_ffn_gate_b, L0_ffn_w1, L0_ffn_b1, L0_ffn_w2, L0_ffn_b2, L0_ffn_w3, L0_ffn_b3, L0_ffn_sw1, L0_ffn_sb1, L0_ffn_sw2, L0_ffn_sb2, L0_ffn_sw3, L0_ffn_sb3)
    return x

_drawn_inputs = setup_inputs


def setup_inputs(seed=0):
    import zlib

    import numpy as np

    out = dict(_drawn_inputs(seed))
    spreads = {'L0_attn_proj_b': (0.0, 0.1),
     'L0_attn_reto_b': (0.0, 0.489),
     'L0_attn_ln1_g': (1.0, 0.6),
     'L0_attn_ln1_b': (0.0, 0.8),
     'L0_attn_ln2_g': (1.0, 0.6),
     'L0_attn_ln2_b': (0.0, 2.0),
     'L0_attn_ffn1_b': (0.0, 1.722),
     'L0_attn_ffn2_b': (0.0, 0.475),
     'L0_attn_lnf_g': (1.0, 0.6),
     'L0_attn_lnf_b': (0.0, 0.717)}
    factors = {'L0_ffn_gate_w': 8.0,
     'L0_ffn_gate_b': 8.0,
     'L0_ffn_w1': 8.0,
     'L0_ffn_b1': 8.0,
     'L0_ffn_w2': 8.0,
     'L0_ffn_b2': 31.982,
     'L0_ffn_w3': 8.0,
     'L0_ffn_b3': 8.0,
     'L0_ffn_sw1': 8.0,
     'L0_ffn_sb1': 8.0,
     'L0_ffn_sw2': 8.0,
     'L0_ffn_sb2': 28.124,
     'L0_ffn_sw3': 8.0,
     'L0_ffn_sb3': 8.0,
     'L0_attn_ffn1_w': 3.809}
    for name, (base, spread) in spreads.items():
        noise = np.random.default_rng([zlib.crc32(name.encode()), seed]).standard_normal(out[name].shape)
        drawn = base * np.exp(spread * noise) if base else spread * noise
        out[name] = jnp.asarray(drawn.astype(out[name].dtype))
    for name, factor in factors.items():
        out[name] = (out[name] * factor).astype(out[name].dtype)
    return out
```

```python
from contextlib import ExitStack

import numpy as np

import concourse.bass as bass
from concourse import mybir

F32 = mybir.dt.float32
ALU = mybir.AluOpType
ACT = mybir.ActivationFunctionType
AX_X = mybir.AxisListType.X

P = 128
N_TOK = 2048
NT = 4
MT = NT * P
MACROS = N_TOK // MT
LAYERS = 2
HEADS = 16
HD = P // HEADS
GROUPS = 4
GH = HEADS // GROUPS
GP = P // GROUPS
FFN = 4
EXPERTS = 8
UNITS = EXPERTS + 2
KB = 2
EPS = 1e-5
SCORES = NT * GROUPS

PER_LAYER = [("ln1_g", 1), ("ln1_b", 1), ("ln2_g", 1), ("ln2_b", 1), ("bq", 1), ("bk", 1), ("bx", 1),
             ("ffn1_b", FFN), ("bv", P), ("reto_b", P), ("ffn2_b", P)]
SMALL = ([("ident", P), ("causal", P), ("decay_q", P), ("decay_k", P), ("same_head", P), ("decay_chunk", 1),
          ("head_mask", GH), ("before", EXPERTS * EXPERTS), ("gate_b", EXPERTS), ("gate_w", EXPERTS),
          ("b1", UNITS * KB), ("b3", UNITS * KB), ("lnf_g", P), ("lnf_b", P), ("sb2", P)]
         + [(f"{n}_{l}", w) for l in range(LAYERS) for n, w in PER_LAYER])
LAYER_W = [("proj", 4 * P), ("reto", P), ("ffn1", FFN * P), ("ffn2", FFN * P)]


def columns(fields):
    at, where = 0, {}
    for name, width in fields:
        where[name] = (at, at + width)
        at += width
    return where, at


STEPS = [("begin",), ("load",), ("norm", 0, 1), ("moe", 0, 0),
         ("turn", 0, 1), ("moe", 0, 1), ("project", 0), ("moe", 1, 0), ("turn_k", 0), ("moe", 1, 1), ("state", 0),
         ("retain", 0), ("moe", 2, 0), ("reto", 0), ("norm", 0, 2), ("moe", 2, 1), ("turn", 0, 2), ("moe", 3, 0),
         ("ffn1", 0), ("next_norm",), ("moe", 3, 1), ("ffn2", 0), ("norm", 1, 1), ("moe", 4, 0), ("next_turn",),
         ("turn", 1, 1), ("moe", 4, 1), ("project", 1), ("next_gate",), ("moe", 5, 0), ("turn_k", 1), ("moe", 5, 1), ("state", 1),
         ("retain", 1), ("moe", 6, 0), ("reto", 1), ("norm", 1, 2), ("next_bias",), ("moe", 6, 1), ("turn", 1, 2), ("moe", 7, 0),
         ("ffn1", 1), ("next_acc",), ("moe", 7, 1), ("ffn2", 1), ("norm", 1, 3), ("moe", 8, 0), ("moe", 8, 1), ("moe", 9, 0), ("moe", 9, 1),
         ("moe_end",), ("finish",)]
NEXT = [("load",), ("next_norm",), ("next_turn",), ("next_gate",), ("next_bias",), ("next_acc",)]

LAST_STEPS = [step for step in STEPS if step not in NEXT]
PHASES = (NEXT, STEPS, LAST_STEPS)


def phase_of(t):
    return 0 if t is None else 2 if isinstance(t, int) else 1


class Count:

    def __init__(self, sem, adds, credit=0):
        self.sem, self.adds, self.credit = sem, adds, credit
        self.before, self.total = [], []
        for steps in PHASES:
            at, n = {}, 0
            for step in steps:
                at[step] = n
                n += self.of(step)
            self.before.append(at)
            self.total.append(n)

    def of(self, step):
        return self.adds.get(step, self.adds.get(step[0], 0))

    def value(self, t, step, n):
        phase = phase_of(t)
        n += self.before[phase][step] + self.credit
        return n if phase == 0 else t * self.total[1] + (self.total[0] + n)

    def wait(self, eng, t, step, n):
        eng.wait_ge(self.sem, self.value(t, step, n))

    def wait_all_before(self, eng, t, step):
        self.wait(eng, t, step, 0)


USES_OF = {"turn": 1, "project": 4, "turn_k": 1, "state": 1, "reto": 1, "ffn1": FFN, "ffn2": 1,
           "next_turn": 1, "next_gate": 1, "next_bias": 1, "next_acc": 1}


class SharedBanks:

    def __init__(self, ready, done):
        self.ready, self.done = Count(ready, USES_OF), done
        assert all(n % 2 == 0 for n in self.ready.total[:2])

    def number(self, t, step, j):
        return self.ready.before[phase_of(t)][step] + j

    def bank(self, t, step, j=0):
        return self.number(t, step, j) % 2

    def wait_product(self, eng, t, step, j=0):
        self.ready.wait(eng, t, step, j + 1)

    def taken(self, t, step, j=0):
        n = self.number(t, step, j) // 2 + 1
        if t is not None:
            n = t * (self.ready.total[1] // 2) + (self.ready.total[0] // 2 + n)
        return self.bank(t, step, j), n

    def wait_taken(self, eng, t, *uses, free=None):
        last = {}
        numbers = [(self.number(t, step, j), step, j, 0) for step, j in uses]
        if free is not None:
            numbers.append((self.number(t, *free) - 2, *free, 1))
        for number, step, j, earlier in sorted(numbers, key=lambda x: x[0]):
            last[number % 2] = (step, j, earlier)
        for step, j, earlier in last.values():
            bank, n = self.taken(t, step, j)
            n = n - earlier
            if t is not None or n > 0:
                eng.wait_ge(self.done[bank], n)


def retention_moe(nc, x, small, layer_w, w1, w3, w2, b2, out):
    where, n_small = columns(SMALL)
    where_w, n_layer = columns(LAYER_W)
    x_v = x.rearrange("a (m i p) d -> (a m) p i d", i=NT, p=P)
    out_v = out.rearrange("a (m i p) d -> (a m) p i d", i=NT, p=P)

    with ExitStack() as ctx:
        def sb(name, shape):
            return ctx.enter_context(nc.sbuf_tensor(name, shape, F32))

        def psum(name, shape):
            return ctx.enter_context(nc.psum_tensor(name, shape, F32))

        def sem(name):
            return ctx.enter_context(nc.semaphore(name))

        small_s = sb("small_s", [P, n_small])
        layer_s = sb("layer_s", [P, LAYERS, n_layer])
        w1_s = sb("w1_s", [P, UNITS, KB * P])
        w3_s = sb("w3_s", [P, UNITS, KB * P])
        w2_s = sb("w2_s", [P, UNITS, KB, P])
        b2_s = sb("b2_s", [EXPERTS, P])
        minus_half = sb("minus_half", [P, NT])
        out_bias = sb("out_bias", [P, P])
        pool_carrier = sb("pool_carrier", [P, 2 * len(STEPS)])
        dve_carrier = sb("dve_carrier", [P, len(STEPS)])

        x_in = sb("x_in", [P, NT, P])
        xn_next = sb("xn_next", [P, NT, P])
        xnT_next = sb("xnT_next", [P, MT])
        cw_next = sb("cw_next", [P, NT, EXPERTS])
        cwT_next = sb("cwT_next", [EXPERTS, MT])
        x_biased = sb("x_biased", [P, NT, P])
        acc_next = sb("acc_next", [P, NT, P])
        stats_next = sb("stats_next", [P, NT, 6])
        mean_var_next = sb("mean_var_next", [P, NT, 2])
        var_eps_next = sb("var_eps_next", [P, NT])
        rstd_next = sb("rstd_next", [P, NT])
        logits = sb("logits", [P, NT, EXPERTS])
        top = sb("top", [P, NT])
        shifted = sb("shifted", [P, NT, EXPERTS])
        exps = sb("exps", [P, NT, EXPERTS])
        above = sb("above", [P, NT, EXPERTS, EXPERTS])
        ties = sb("ties", [P, NT, EXPERTS, EXPERTS])
        rank = sb("rank", [P, NT, EXPERTS])
        chosen = sb("chosen", [P, NT, EXPERTS])
        exps_sum = sb("exps_sum", [P, NT])
        chosen_sum = sb("chosen_sum", [P, NT])
        scale = sb("scale", [P, NT])

        res = sb("res", [P, NT, P])
        xnT = sb("xnT", [P, MT])
        cw = sb("cw", [P, NT, EXPERTS])
        acc = sb("acc", [P, NT, P])
        stats = sb("stats", [P, NT, 6])
        mean_var = sb("mean_var", [P, NT, 2])
        var_eps = sb("var_eps", [P, NT])
        rstd = sb("rstd", [P, NT])
        normed = sb("normed", [P, NT, P])
        hT = sb("hT", [P, MT])
        qT = sb("qT", [P, NT, P])
        q_heads = sb("q_heads", [P, NT, GH, P])
        kT = sb("kT", [P, NT, P])
        k_tok = sb("k_tok", [P, NT, P])
        v_tok = sb("v_tok", [P, NT, P])
        v_heads = sb("v_heads", [P, NT, GROUPS, GH * GP])
        gateT = sb("gateT", [P, MT])
        retT = sb("retT", [P, MT])
        scores = sb("scores", [P, 2, GH, P])
        chunk_kv = sb("chunk_kv", [P, NT, P])
        state = sb("state", [P, LAYERS, NT, P])
        gelus = sb("gelus", [P, FFN, MT])
        silus = sb("silus", [P, 2, MT])
        hidden = sb("hidden", [P, 2, KB, MT])
        final = sb("final", [P, NT, P])
        out_s = sb("out_s", [P, NT, P])

        shared_p = psum("shared_p", [P, 2, MT])
        scores_p = psum("scores_p", [P, 2, MT])
        ret_p = psum("ret_p", [P, MT])
        up_p = psum("up_p", [P, 2, MT])
        down_p = psum("down_p", [P, MT])

        def col(name, l=None):
            a, b = where[name if l is None else f"{name}_{l}"]
            return small_s[:, a:b]

        def over(ap, n=NT):
            return ap.unsqueeze(1).broadcast_to([P, n, ap.shape[-1]])

        def weight(name, l):
            a, b = where_w[name]
            return layer_s[:, l, a:b]

        def tiles(ap):
            return ap.rearrange("p (i n) -> p i n", i=NT)

        def tile_of(ap, i):
            return ap[:, i * P:(i + 1) * P]

        s_small, s_layer, s_w1, s_w3, s_w2, s_b2 = [sem(f"{n}_loaded") for n in ("small", "layer_w", "w1", "w3", "w2", "b2")]
        s_x = sem("x_loaded")
        s_filled = sem("constants_filled")
        s_out_bias = sem("out_bias_ready")
        s_stored = sem("out_stored")

        x_biased_ready = Count(sem("x_biased_ready"), {"next_norm": 1})
        var_next_ready = Count(sem("var_next_ready"), {"next_norm": 1})
        rstd_next_ready = Count(sem("rstd_next_ready"), {"next_norm": 1})
        xn_next_ready = Count(sem("xn_next_ready"), {"next_norm": 1})
        shifted_ready = Count(sem("shifted_ready"), {"next_gate": 1})
        exps_ready = Count(sem("exps_ready"), {"next_gate": 1})
        cw_next_ready = Count(sem("cw_next_ready"), {"next_gate": 1})
        begun = Count(sem("begin_copies"), {"begin": 3})
        xnT_ready = Count(sem("xnT_ready"), {"begin": 1})
        var_ready = Count(sem("var_ready"), {"norm": 1})
        rstd_ready = Count(sem("rstd_ready"), {"norm": 1})
        normed_ready = Count(sem("normed_ready"), {"norm": 1})
        res_biased = Count(sem("res_biased"), {"norm": 1})
        q_heads_ready = Count(sem("q_heads_ready"), {"project": 1})
        v_heads_ready = Count(sem("v_heads_ready"), {"project": 1})
        state_ready = Count(sem("state_ready"), {"state": NT - 1, "retain": 1}, credit=1)
        scored = Count(sem("scores_in_psum"), {"retain": SCORES})
        masked = Count(sem("scores_masked"), {"retain": SCORES})
        retained = Count(sem("retention_in_psum"), {"retain": 1})
        gated = Count(sem("retention_gated"), {"retain": 1})
        w1_ready = Count(sem("w1_product"), {"moe": 1})
        w3_ready = Count(sem("w3_product"), {"moe": 1})
        silu_ready = Count(sem("silu_ready"), {"moe": 1}, credit=1)
        hidden_ready = Count(sem("hidden_ready"), {"moe": 1}, credit=2)
        down_steps = {("moe", u, 0): 1 for u in range(1, UNITS)} | {("moe_end",): 1}
        down_ready = Count(sem("down_product"), down_steps, credit=1)
        acc_updated = Count(sem("acc_updated"), down_steps, credit=1)
        out_ready = Count(sem("out_ready"), {"finish": 1}, credit=1)
        pool_link = Count(sem("pool_link"), {"norm": 1, "next_norm": 1})
        dve_link = Count(sem("vector_link"), {"norm": 1, "next_norm": 1, "next_gate": 9})
        shared = SharedBanks(sem("shared_product"), [sem("shared_taken_0"), sem("shared_taken_1")])

        def run(eng, step_of):
            for step in NEXT:
                step_of(None, step)
            with eng.Fori(0, MACROS - 1) as t:
                for step in STEPS:
                    step_of(t, step)
            for step in LAST_STEPS:
                step_of(MACROS - 1, step)

        block = ctx.enter_context(nc.Block())

        @block.sync
        def _(sp):
            sp.dma_start(x_in[:], x_v[0, :, :, :]).then_inc(s_x, 16)
            sp.dma_start(layer_s[:], layer_w).then_inc(s_layer, 16)
            sp.dma_start(w1_s[:], w1).then_inc(s_w1, 16)
            sp.dma_start(w2_s[:], w2).then_inc(s_w2, 16)

            def step_of(t, step):
                if step[0] == "load" and t is not None:
                    xn_next_ready.wait_all_before(sp, t, step)
                    x_biased_ready.wait_all_before(sp, t, step)
                    sp.dma_start(x_in[:], x_v[t + 1, :, :, :]).then_inc(s_x, 16)
                if step[0] == "finish":
                    out_ready.wait(sp, t, step, 1)
                    sp.dma_start(out_v[t, :, :, :], out_s[:]).then_inc(s_stored, 16)

            run(sp, step_of)
            sp.wait_ge(s_stored, 16 * (MACROS + 1))

        @block.gpsimd
        def _(pool):
            pool.memset(minus_half[:], -0.5).then_inc(s_filled, 1)
            pool.memset(state[:], 0.0).then_inc(state_ready.sem, 1)
            pool.memset(v_heads[:], 0.0).then_inc(s_filled, 1)
            pool.wait_ge(s_small, 16)
            pool.tensor_tensor(out_bias[:], col("lnf_b"), col("sb2"), ALU.add).then_inc(s_out_bias, 1)
            pool.wait_ge(s_filled, 2)
            pool.wait_ge(s_out_bias, 1)

            def carry_wait(step, n=0):
                c = 2 * STEPS.index(step) + n
                pool.tensor_tensor(pool_carrier[:, c:c + 1], minus_half[:, 0:1], minus_half[:, 0:1], ALU.mult)

            def inverse_std(t, step, variance, var_eps, done, to):
                carry_wait(step)
                pool.tensor_scalar(var_eps[:], variance, EPS, None, ALU.add).then_inc(pool_link.sem, 1)
                pool_link.wait(pool, t, step, 1)
                pool.tensor_tensor(to[:], var_eps[:], minus_half[:], ALU.pow).then_inc(done.sem, 1)

            def step_of(t, step):
                kind = step[0]
                if kind == "begin":
                    out_ready.wait_all_before(pool, t, step)
                    carry_wait(step)
                    pool.tensor_copy(res[:], xn_next[:]).then_inc(begun.sem, 1)
                    acc_updated.wait_all_before(pool, t, step)
                    carry_wait(step, 1)
                    pool.tensor_copy(cw[:], cw_next[:]).then_inc(begun.sem, 1)
                    pool.tensor_copy(acc[:], acc_next[:]).then_inc(begun.sem, 1)
                elif kind == "next_norm":
                    pool.wait_ge(s_x, 16 if t is None else t * 16 + 32)
                    pool.tensor_tensor(x_biased[:], x_in[:], over(out_bias[:]), ALU.add).then_inc(x_biased_ready.sem, 1)
                    var_next_ready.wait(pool, t, step, 1)
                    inverse_std(t, step, mean_var_next[:, :, 1], var_eps_next, rstd_next_ready, rstd_next)
                elif kind == "norm":
                    l, w = step[1:]
                    var_ready.wait(pool, t, step, 1)
                    inverse_std(t, step, mean_var[:, :, 1], var_eps, rstd_ready, rstd)
                    normed_ready.wait(pool, t, step, 1)
                    if w == 3:
                        pool.tensor_tensor(final[:], normed[:], over(col("lnf_g")), ALU.mult).then_inc(res_biased.sem, 1)
                    else:
                        bias = col("reto_b" if w == 1 else "ffn2_b", l)
                        pool.tensor_tensor(res[:], res[:], over(bias), ALU.add).then_inc(res_biased.sem, 1)
                elif kind == "project":
                    l = step[1]
                    shared.wait_taken(pool, t, (step, 0))
                    carry_wait(step)
                    for j in range(GH):
                        ins = pool.tensor_scalar(q_heads[:, :, j, :], qT[:], col("head_mask")[:, j:j + 1], None, ALU.mult)
                    ins.then_inc(q_heads_ready.sem, 1)
                    shared.wait_taken(pool, t, (step, 3))
                    carry_wait(step, 1)
                    for i in range(NT):
                        own = v_heads[:, i].rearrange("p g (b e) -> p g b e", e=HD)[:, :, 0:GH * GH:GH + 1, :]
                        ins = pool.tensor_copy(own, v_tok[:, i].rearrange("p (g j e) -> p g j e", g=GROUPS, e=HD))
                    ins.then_inc(v_heads_ready.sem, 1)

            run(pool, step_of)

        @block.scalar
        def _(act):
            act.dma_start(small_s[:], small).then_inc(s_small, 16)
            act.dma_start(b2_s[:], b2).then_inc(s_b2, 16)
            act.dma_start(w3_s[:], w3).then_inc(s_w3, 16)
            act.wait_ge(s_small, 16)
            act.activation(silus[:, 0, 0:1], col("ident")[:, 0:1], ACT.Silu).then_inc(silu_ready.sem, 1)

            def take(t, step, j, to, func=ACT.Copy, **more):
                shared.wait_product(act, t, step, j)
                bank = shared.bank(t, step, j)
                return act.activation(to, shared_p[0:to.shape[0], bank, :], func, **more).then_inc(shared.done[bank], 1)

            def step_of(t, step):
                kind = step[0]
                if kind == "begin":
                    down_ready.wait_all_before(act, t, step)
                    act.activation(xnT[:], xnT_next[:], ACT.Copy).then_inc(xnT_ready.sem, 1)
                elif kind == "next_turn":
                    if t is not None:
                        xnT_ready.wait_all_before(act, t, step)
                    take(t, step, 0, xnT_next[:])
                elif kind == "next_gate":
                    shifted_ready.wait(act, t, step, 1)
                    act.activation(exps[:], shifted[:], ACT.Exp).then_inc(exps_ready.sem, 1)
                elif kind == "next_bias":
                    take(t, step, 0, cwT_next[:])
                elif kind == "turn":
                    l, w = step[1:]
                    take(t, step, 0, hT[:], ACT.Identity, scale=col(f"ln{w}_g", l), bias=col(f"ln{w}_b", l))
                elif kind == "project":
                    take(t, step, 2, gateT[:], ACT.Silu, bias=col("bx", step[1]))
                elif kind == "turn_k":
                    take(t, step, 0, k_tok[:].rearrange("p i n -> p (i n)"))
                elif kind == "ffn1":
                    for f in range(FFN):
                        take(t, step, f, gelus[:, f, :], ACT.Gelu, bias=col("ffn1_b", step[1])[:, f:f + 1])
                elif kind == "moe":
                    u, k = step[1:]
                    w1_ready.wait(act, t, step, 1)
                    hidden_ready.wait(act, t, step, -1)
                    act.activation(silus[:, k, :], up_p[:, 0, :], ACT.Silu,
                                   bias=col("b1")[:, u * KB + k:u * KB + k + 1]).then_inc(silu_ready.sem, 1)

            run(act, step_of)

        @block.vector
        def _(dve):
            dve.memset(stats[:], 0.0).then_inc(hidden_ready.sem, 2)
            dve.memset(mean_var[:], 0.0).then_inc(acc_updated.sem, 1)
            dve.memset(rank[:], 0.0).then_inc(s_stored, 16)
            dve.wait_ge(s_small, 16)
            linked = [None, 0]

            def link(t, step, ins):
                if linked[0] != (phase_of(t), step):
                    linked[:] = [(phase_of(t), step), 0]
                linked[1] += 1
                ins.then_inc(dve_link.sem, 1)
                dve_link.wait(dve, t, step, linked[1])

            def normalise(t, step, rows, stats, mean_var, rstd, to, var_done, rstd_done, done):
                for i in range(NT):
                    ins = dve.bn_stats(stats[:, i, :], rows[:, i, :])
                link(t, step, ins)
                c = STEPS.index(step)
                dve.memset(dve_carrier[:, c:c + 1], 0.0)
                for i in range(NT):
                    ins = dve.bn_aggr(mean_var[:, i, :], stats[:, i, :])
                ins.then_inc(var_done.sem, 1)
                rstd_done.wait(dve, t, step, 1)
                for i in range(NT):
                    ins = dve.tensor_scalar(to[:, i, :], rows[:, i, :], mean_var[:, i, 0:1], rstd[:, i:i + 1],
                                            ALU.subtract, ALU.mult)
                ins.then_inc(done.sem, 1)

            def product(t, step, j=0):
                shared.wait_product(dve, t, step, j)
                return shared_p[:, shared.bank(t, step, j), :]

            def taken(t, step, j, ins):
                ins.then_inc(shared.done[shared.bank(t, step, j)], 1)

            def gate(t, step):
                p = product(t, step)[:, 0:NT * EXPERTS].rearrange("p (i e) -> p i e", e=EXPERTS)
                if t is not None:
                    begun.wait_all_before(dve, t, step)
                taken(t, step, 0, dve.tensor_tensor(logits[:], p, over(col("gate_b")), ALU.add))
                shared.wait_taken(dve, t, (step, 0))
                mine = logits[:].unsqueeze(3).broadcast_to([P, NT, EXPERTS, EXPERTS])
                other = logits[:].unsqueeze(2).broadcast_to([P, NT, EXPERTS, EXPERTS])
                link(t, step, dve.tensor_reduce(top[:], logits[:], AX_X, ALU.max))
                dve.tensor_tensor(shifted[:], logits[:], top[:].unsqueeze(2).broadcast_to([P, NT, EXPERTS]),
                                  ALU.subtract).then_inc(shifted_ready.sem, 1)
                dve.tensor_tensor(above[:], other, mine, ALU.is_gt)
                link(t, step, dve.tensor_tensor(ties[:], other, mine, ALU.is_equal))
                flat = "p i a b -> p i (a b)"
                link(t, step, dve.tensor_tensor(ties[:].rearrange(flat), ties[:].rearrange(flat), over(col("before")), ALU.mult))
                link(t, step, dve.tensor_tensor(above[:], above[:], ties[:], ALU.add))
                link(t, step, dve.tensor_reduce(rank[:], above[:], AX_X, ALU.add))
                exps_ready.wait(dve, t, step, 1)
                dve.tensor_reduce(exps_sum[:], exps[:], AX_X, ALU.add)
                link(t, step, dve.scalar_tensor_tensor(out=chosen[:], in0=rank[:], scalar=1.5, in1=exps[:],
                                                       op0=ALU.is_lt, op1=ALU.mult))
                link(t, step, dve.tensor_reduce(chosen_sum[:], chosen[:], AX_X, ALU.add))
                link(t, step, dve.scalar_tensor_tensor(out=chosen_sum[:], in0=exps_sum[:], scalar=1e-20, in1=chosen_sum[:],
                                                       op0=ALU.mult, op1=ALU.add))
                link(t, step, dve.reciprocal(scale[:], chosen_sum[:]))
                dve.tensor_tensor(cw_next[:], chosen[:], scale[:].unsqueeze(2).broadcast_to([P, NT, EXPERTS]),
                                  ALU.mult).then_inc(cw_next_ready.sem, 1)

            def add_to_acc(t, step, u):
                down_ready.wait(dve, t, step, 1)
                if u == 0:
                    begun.wait(dve, t, ("begin",), 3)
                acc_updated.wait(dve, t, step, 0)
                if u < EXPERTS:
                    for i in range(NT):
                        ins = dve.scalar_tensor_tensor(out=acc[:, i, :], in0=tile_of(down_p, i), scalar=cw[:, i, u:u + 1],
                                                       in1=acc[:, i, :], op0=ALU.mult, op1=ALU.add)
                else:
                    ins = dve.tensor_tensor(acc[:], tiles(down_p[:]), acc[:], ALU.add)
                ins.then_inc(acc_updated.sem, 1)

            def step_of(t, step):
                kind = step[0]
                if kind == "next_norm":
                    dve.wait_ge(s_x, 16 if t is None else t * 16 + 32)
                    if t is not None:
                        begun.wait(dve, t, ("begin",), 1)
                    normalise(t, step, x_in, stats_next, mean_var_next, rstd_next, xn_next,
                              var_next_ready, rstd_next_ready, xn_next_ready)
                elif kind == "next_gate":
                    gate(t, step)
                elif kind == "next_acc":
                    x_biased_ready.wait(dve, t, ("next_norm",), 1)
                    taken(t, step, 0, dve.tensor_tensor(acc_next[:], tiles(product(t, step)), x_biased[:], ALU.add))
                    if t is None:
                        dve.memset(out_s[:], 0.0).then_inc(out_ready.sem, 1)
                elif kind == "norm":
                    l, w = step[1:]
                    if (l, w) == (0, 1):
                        begun.wait(dve, t, ("begin",), 1)
                    else:
                        shared.wait_taken(dve, t, (("reto", l) if w == 2 else ("ffn2", l - 1 if w == 1 else l), 0))
                    normalise(t, step, res, stats, mean_var, rstd, normed, var_ready, rstd_ready, normed_ready)
                elif kind == "project":
                    l = step[1]
                    for j, (to, bias, decay) in enumerate(((qT, "bq", "decay_q"), (kT, "bk", "decay_k"))):
                        taken(t, step, j, dve.scalar_tensor_tensor(out=to[:], in0=tiles(product(t, step, j)), scalar=col(bias, l),
                                                                   in1=over(col(decay)), op0=ALU.add, op1=ALU.mult))
                    taken(t, step, 3, dve.tensor_tensor(v_tok[:], tiles(product(t, step, 3)), over(col("bv", l)), ALU.add))
                elif kind == "state":
                    l = step[1]
                    taken(t, step, 0, dve.scalar_tensor_tensor(out=chunk_kv[:], in0=tiles(product(t, step)), scalar=col("decay_chunk"),
                                                               in1=over(col("same_head")), op0=ALU.mult, op1=ALU.mult))
                    shared.wait_taken(dve, t, (step, 0))
                    for i in range(NT - 1):
                        state_ready.wait(dve, t, step, i)
                        next_state(l, i)
                elif kind == "retain":
                    l = step[1]
                    for n in range(SCORES):
                        scored.wait(dve, t, step, n + 1)
                        dve.tensor_tensor(scores[:, n % 2], scores_p[:, n % 2, :].rearrange("p (j n) -> p j n", j=GH),
                                          over(col("causal"), GH), ALU.mult).then_inc(masked.sem, 1)
                    retained.wait(dve, t, step, 1)
                    shared.wait_taken(dve, t, (("project", l), 2))
                    dve.tensor_tensor(retT[:], ret_p[:], gateT[:], ALU.mult).then_inc(gated.sem, 1)
                    state_ready.wait(dve, t, step, 0)
                    next_state(l, NT - 1)
                elif kind in ("reto", "ffn2"):
                    l = step[1]
                    norm = ("norm", l, 1 if kind == "reto" else 2)
                    res_biased.wait(dve, t, norm, 1)
                    taken(t, step, 0, dve.tensor_tensor(res[:], tiles(product(t, step)), res[:], ALU.add))
                elif kind == "moe":
                    u, k = step[1:]
                    silu_ready.wait(dve, t, step, 1)
                    w3_ready.wait(dve, t, step, 1)
                    b = u * KB + k
                    dve.scalar_tensor_tensor(out=hidden[:, u % 2, k, :], in0=up_p[:, 1, :], scalar=col("b3")[:, b:b + 1],
                                             in1=silus[:, k, :], op0=ALU.add, op1=ALU.mult).then_inc(hidden_ready.sem, 1)
                    if k == 0 and u > 0:
                        add_to_acc(t, step, u - 1)
                elif kind == "moe_end":
                    add_to_acc(t, step, UNITS - 1)
                elif kind == "finish":
                    res_biased.wait(dve, t, ("norm", LAYERS - 1, 3), 1)
                    acc_updated.wait(dve, t, ("moe_end",), 1)
                    dve.wait_ge(s_stored, t * 16 + 16)
                    dve.tensor_tensor(out_s[:], final[:], acc[:], ALU.add).then_inc(out_ready.sem, 1)

            def next_state(l, i):
                dve.scalar_tensor_tensor(out=state[:, l, (i + 1) % NT], in0=state[:, l, i], scalar=col("decay_chunk"),
                                         in1=chunk_kv[:, i], op0=ALU.mult, op1=ALU.add).then_inc(state_ready.sem, 1)

            run(dve, step_of)

        @block.tensor
        def _(pe):
            pe.wait_ge(s_small, 16)
            shared_ready = shared.ready.sem

            def use(t, step, j=0, of=()):
                shared.wait_taken(pe, t, *of, free=(step, j))
                return shared_p[:, shared.bank(t, step, j), :]

            def turn(to, rows):
                for i in range(NT):
                    ins = pe.transpose(tile_of(to, i)[0:rows.shape[2], :], rows[:, i, :], col("ident"))
                ins.then_inc(shared_ready, 1)

            def tokens_product(to, lhs, rhs):
                n = rhs[0].shape[-1]
                for i in range(NT):
                    for b, (left, right) in enumerate(zip(lhs, rhs)):
                        ins = pe.matmul(to[:, i * n:(i + 1) * n], tile_of(left, i), right,
                                        start=(b == 0), stop=(b == len(rhs) - 1))
                return ins

            def retain(t, step):
                l = step[1]
                q_heads_ready.wait(pe, t, ("project", l), 1)
                v_heads_ready.wait(pe, t, ("project", l), 1)

                def score(n):
                    i, g = divmod(n, GROUPS)
                    rows = slice(g * GP, (g + 1) * GP)
                    pe.matmul(scores_p[:, n % 2, :], kT[rows, i, :], q_heads[rows, i].rearrange("p j n -> p (j n)"),
                              start=True, stop=True).then_inc(scored.sem, 1)

                score(0)
                for n in range(SCORES):
                    i, g = divmod(n, GROUPS)
                    if n + 1 < SCORES:
                        score(n + 1)
                    if g == 0:
                        state_ready.wait(pe, t, ("state", l), i)
                        pe.matmul(tile_of(ret_p, i), state[:, l, i], qT[:, i], start=True, stop=False, skip_group_check=True)
                    masked.wait(pe, t, step, n + 1)
                    for j in range(GH):
                        ins = pe.matmul(ret_p[g * GP:(g + 1) * GP, i * P:(i + 1) * P], v_heads[:, i, g, j * GP:(j + 1) * GP],
                                        scores[:, n % 2, j, :], start=False, stop=True, skip_group_check=True)
                ins.then_inc(retained.sem, 1)

            def step_of(t, step):
                kind = step[0]
                if kind == "next_turn":
                    xn_next_ready.wait(pe, t, ("next_norm",), 1)
                    turn(use(t, step), xn_next)
                elif kind == "next_gate":
                    to = use(t, step, of=[(("next_turn",), 0)])
                    tokens_product(to, [xnT_next], [col("gate_w")]).then_inc(shared_ready, 1)
                elif kind == "next_bias":
                    cw_next_ready.wait(pe, t, ("next_gate",), 1)
                    turn(use(t, step), cw_next)
                elif kind == "next_acc":
                    to = use(t, step, of=[(("next_bias",), 0)])
                    pe.wait_ge(s_b2, 16)
                    tokens_product(to, [cwT_next], [b2_s[:]]).then_inc(shared_ready, 1)
                    if t is None:
                        pe.transpose(down_p[:, 0:P], col("ident"), col("ident")).then_inc(down_ready.sem, 1)
                elif kind == "turn":
                    normed_ready.wait(pe, t, ("norm", *step[1:]), 1)
                    turn(use(t, step), normed)
                elif kind == "project":
                    l = step[1]
                    pe.wait_ge(s_layer, 16)
                    for j, block_of in enumerate((0, 1, 3)):
                        to = use(t, step, j, of=[(("turn", l, 1), 0)])
                        pe.matmul(to, tile_of(weight("proj", l), block_of), hT[:], start=True, stop=True).then_inc(shared_ready, 1)
                    tokens_product(use(t, step, 3), [hT], [tile_of(weight("proj", l), 2)]).then_inc(shared_ready, 1)
                elif kind == "turn_k":
                    turn(use(t, step, of=[(("project", step[1]), 1)]), kT)
                elif kind == "state":
                    l = step[1]
                    to = use(t, step, of=[(("turn_k", l), 0), (("project", l), 3)])
                    for i in range(NT):
                        ins = pe.matmul(tile_of(to, i), k_tok[:, i], v_tok[:, i], start=True, stop=True)
                    ins.then_inc(shared_ready, 1)
                elif kind == "retain":
                    retain(t, step)
                elif kind == "reto":
                    gated.wait(pe, t, ("retain", step[1]), 1)
                    tokens_product(use(t, step), [retT], [weight("reto", step[1])]).then_inc(shared_ready, 1)
                elif kind == "ffn1":
                    l = step[1]
                    for f in range(FFN):
                        to = use(t, step, f, of=[(("turn", l, 2), 0)])
                        pe.matmul(to, tile_of(weight("ffn1", l), f), hT[:], start=True, stop=True).then_inc(shared_ready, 1)
                elif kind == "ffn2":
                    l = step[1]
                    to = use(t, step, of=[(("ffn1", l), f) for f in range(FFN)])
                    tokens_product(to, [gelus[:, f, :] for f in range(FFN)],
                                   [tile_of(weight("ffn2", l), f) for f in range(FFN)]).then_inc(shared_ready, 1)
                elif kind == "moe":
                    u, k = step[1:]
                    if (u, k) == (0, 0):
                        xnT_ready.wait(pe, t, ("begin",), 1)
                        pe.wait_ge(s_w1, 16)
                        pe.wait_ge(s_w3, 16)
                    silu_ready.wait(pe, t, step, 0)
                    pe.matmul(up_p[:, 0, :], tile_of(w1_s[:, u], k), xnT[:], start=True, stop=True).then_inc(w1_ready.sem, 1)
                    hidden_ready.wait(pe, t, step, 0)
                    pe.matmul(up_p[:, 1, :], tile_of(w3_s[:, u], k), xnT[:], start=True, stop=True).then_inc(w3_ready.sem, 1)
                    if k == 0 and u > 0:
                        down(t, step, u - 1)
                elif kind == "moe_end":
                    down(t, step, UNITS - 1)

            def down(t, step, u):
                if u == 0:
                    pe.wait_ge(s_w2, 16)
                hidden_ready.wait(pe, t, ("moe", u, KB - 1), 1)
                acc_updated.wait(pe, t, step, 0)
                tokens_product(down_p, [hidden[:, u % 2, k] for k in range(KB)],
                               [w2_s[:, u, k] for k in range(KB)]).then_inc(down_ready.sem, 1)

            run(pe, step_of)


IN_NAMES = ["L0_attn_x", "small", "layer_w", "w1", "w3", "w2", "b2"]


def decays():
    gamma = 1.0 - 2.0 ** (-5.0 - np.arange(HEADS))
    by_row = np.repeat(gamma, HD)[:, None]
    n = np.arange(P)[None, :]
    return (by_row ** n).astype(np.float32), (by_row ** -n).astype(np.float32), (by_row ** P).astype(np.float32)


def laid_out(a):
    a = {name: np.asarray(value) for name, value in a.items()}
    rows = lambda v: np.broadcast_to(v.reshape(1, -1), (P, v.size))
    cols = lambda v: v.reshape(-1, P).T
    decay_q, decay_k, decay_chunk = decays()
    r = np.arange(P)
    e = np.arange(EXPERTS)
    f = {
        "ident": np.eye(P, dtype=np.float32),
        "causal": (r[None, :] >= r[:, None]).astype(np.float32),
        "decay_q": decay_q, "decay_k": decay_k, "decay_chunk": decay_chunk,
        "same_head": (r[None, :] // HD == r[:, None] // HD).astype(np.float32),
        "head_mask": ((r[:, None] // HD) % GH == np.arange(GH)[None, :]).astype(np.float32),
        "before": rows((e[None, :] < e[:, None]).astype(np.float32)),
        "gate_b": rows(a["L0_ffn_gate_b"]), "gate_w": a["L0_ffn_gate_w"].T,
        "b1": np.concatenate([cols(a["L0_ffn_b1"]), cols(a["L0_ffn_sb1"])], 1),
        "b3": np.concatenate([cols(a["L0_ffn_b3"]), cols(a["L0_ffn_sb3"])], 1),
        "lnf_g": rows(a["L0_attn_lnf_g"]), "lnf_b": rows(a["L0_attn_lnf_b"]), "sb2": rows(a["L0_ffn_sb2"]),
    }
    for l in range(LAYERS):
        bq, bk, bv, bx = a["L0_attn_proj_b"][l].reshape(4, P)
        f |= {f"ln1_g_{l}": cols(a["L0_attn_ln1_g"][l]), f"ln1_b_{l}": cols(a["L0_attn_ln1_b"][l]),
              f"ln2_g_{l}": cols(a["L0_attn_ln2_g"][l]), f"ln2_b_{l}": cols(a["L0_attn_ln2_b"][l]),
              f"bq_{l}": cols(bq), f"bk_{l}": cols(bk), f"bx_{l}": cols(bx), f"bv_{l}": rows(bv),
              f"ffn1_b_{l}": cols(a["L0_attn_ffn1_b"][l]), f"reto_b_{l}": rows(a["L0_attn_reto_b"][l]),
              f"ffn2_b_{l}": rows(a["L0_attn_ffn2_b"][l])}
    small = np.concatenate([f[name] for name, _ in SMALL], 1)
    by_in = lambda w: w.reshape(LAYERS, -1, P, w.shape[-1]).transpose(2, 0, 1, 3).reshape(P, LAYERS, -1)
    layer_w = np.concatenate([by_in(a[f"L0_attn_{n}_w"]) for n, _ in LAYER_W], 2)
    up = lambda w, sw: np.concatenate([w.transpose(2, 0, 1), sw.reshape(UNITS - EXPERTS, KB * P, P).transpose(2, 0, 1)], 1)
    w2, sw2 = a["L0_ffn_w2"], a["L0_ffn_sw2"]
    down = np.concatenate([w2.reshape(EXPERTS, P, KB, P).transpose(3, 0, 2, 1),
                           sw2.reshape(P, UNITS - EXPERTS, KB, P).transpose(3, 1, 2, 0)], 1)
    return {"L0_attn_x": a["L0_attn_x"], "small": small, "layer_w": layer_w, "w1": up(a["L0_ffn_w1"], a["L0_ffn_sw1"]),
            "w3": up(a["L0_ffn_w3"], a["L0_ffn_sw3"]), "w2": down, "b2": a["L0_ffn_b2"]}


def kernel(**inputs):
    import concourse.bacc as bacc
    from concourse.bass_utils import run_bass_kernel_spmd

    nc = bacc.Bacc("TRN2", target_bir_lowering=False, num_devices=1)
    arrays, args = {}, []
    placed = laid_out(inputs)
    for name in IN_NAMES:
        arrays[f"in_{name}"] = np.ascontiguousarray(placed[name])
        args.append(nc.dram_tensor(f"in_{name}", arrays[f"in_{name}"].shape, F32, kind="ExternalInput").ap())
    args.append(nc.dram_tensor("out", (1, N_TOK, P), F32, kind="ExternalOutput").ap())
    retention_moe(nc, *args)
    r = run_bass_kernel_spmd(nc, [arrays], core_ids=[0])
    return r.results[0]["out"]
```

```python
from contextlib import ExitStack

import numpy as np

import concourse.bass as bass
from concourse import mybir

F32 = mybir.dt.float32
F32R = mybir.dt.float32r
ALU = mybir.AluOpType
ACT = mybir.ActivationFunctionType
AX_X = mybir.AxisListType.X

P = 128
N_TOK = 2048
NT = 4
MT = NT * P
MACROS = N_TOK // MT
LAYERS = 2
HEADS = 16
HD = P // HEADS
GROUPS = 4
GH = HEADS // GROUPS
GP = P // GROUPS
FFN = 4
EXPERTS = 8
UNITS = EXPERTS + 2
KB = 2
EPS = 1e-5

PER_LAYER = [("ln1_g", 1), ("ln1_b", 1), ("ln2_g", 1), ("ln2_b", 1), ("bq", 1), ("bk", 1), ("bx", 1),
             ("ffn1_b", FFN), ("bv", P), ("reto_b", P), ("ffn2_b", P)]
SMALL = ([("ident", P), ("causal", P), ("decay_q", P), ("decay_k", P), ("same_head", P), ("decay_chunk", 1),
          ("head_mask", GH), ("before", EXPERTS * EXPERTS), ("gate_b", EXPERTS), ("gate_w", EXPERTS),
          ("b1", UNITS * KB), ("b3", UNITS * KB), ("lnf_g", P), ("lnf_b", P), ("sb2", P)]
         + [(f"{n}_{l}", w) for l in range(LAYERS) for n, w in PER_LAYER])
LAYER_W = [("proj", 4 * P), ("reto", P), ("ffn1", FFN * P), ("ffn2", FFN * P)]


def columns(fields):
    at, where = 0, {}
    for name, width in fields:
        where[name] = (at, at + width)
        at += width
    return where, at


MOE = "moe"


def retention_steps(l):
    return [("stack", l, 0), MOE, ("stack", l, 1), ("score", l, 0, 0), ("turn_k", l), ("score", l, 0, 1), ("pv", l, 0, 0),
            MOE, ("stack", l, 2), ("score", l, 1, 0), ("pv", l, 0, 1), ("state", l), ("score", l, 1, 1), ("pv", l, 1, 0), MOE,
            ("stack", l, 3), ("score", l, 2, 0), ("pv", l, 1, 1), MOE, ("score", l, 2, 1), ("pv", l, 2, 0),
            MOE, ("score", l, 3, 0), ("pv", l, 2, 1), ("score", l, 3, 1), ("pv", l, 3, 0), ("pv", l, 3, 1), ("inter", l),
            MOE, ("reto", l)]


def numbered(steps):
    halves = iter([("moe", u, k) for u in range(UNITS) for k in range(KB)])
    steps = [next(halves) if step is MOE else step for step in steps]
    return steps + list(halves)


STEPS = numbered(
    [("begin",), ("load",)] + retention_steps(0)
    + [("norm", 0, 2), MOE, MOE, ("turn", 0, 2), MOE, ("ffn1", 0), ("next_norm",), ("ffn2", 0),
       ("norm", 1, 1), MOE, ("next_turn",), ("next_gate",), ("turn", 1, 1), MOE, ("project", 1), MOE]
    + retention_steps(1)
    + [("norm", 1, 2), ("next_bias",), MOE, MOE, ("turn", 1, 2), ("norm", 0, 1), ("ffn1", 1), ("turn", 0, 1), ("ffn2", 1),
       ("norm", 1, 3), ("next_acc",), ("project", 0)]) + [("moe_end",), ("finish",)]
NEXT = [("load",), ("next_norm",), ("next_turn",), ("next_gate",), ("next_bias",), ("norm", 0, 1), ("turn", 0, 1),
        ("next_acc",), ("project", 0)]
assert [step for step in STEPS if step in NEXT] == NEXT
LAST_STEPS = [step for step in STEPS if step not in NEXT]
PHASES = (NEXT, STEPS, LAST_STEPS)


def phase_of(t):
    return 0 if t is None else 2 if isinstance(t, int) else 1


def projected(l):
    return ("project", l) if l > 0 else ("made", "project", l)


class Count:

    def __init__(self, sem, adds, credit=0):
        self.sem, self.adds, self.credit = sem, adds, credit
        self.before, self.total = [], []
        for steps in PHASES:
            at, n = {}, 0
            for step in steps:
                at[step] = n
                n += self.of(step)
            self.before.append(at)
            self.total.append(n)

    def of(self, step):
        return self.adds.get(step, self.adds.get(step[0], 0))

    def steps_before(self, t, step):
        if step[0] != "made":
            return self.before[phase_of(t)][step]
        step = step[1:]
        left = self.total[1] - self.before[1][step]
        assert phase_of(t) > 0 and left == self.total[0] - self.before[0][step]
        return -left

    def value(self, t, step, n):
        phase = phase_of(t)
        n += self.steps_before(t, step) + self.credit
        return n if phase == 0 else t * self.total[1] + (self.total[0] + n)

    def wait(self, eng, t, step, n):
        eng.wait_ge(self.sem, self.value(t, step, n))

    def wait_all_before(self, eng, t, step):
        self.wait(eng, t, step, 0)


USES_OF = {"turn": 1, "project": 4, "stack": 2, "turn_k": 1, "state": 1, "reto": 1, "ffn1": FFN, "ffn2": 1,
           "next_turn": 1, "next_gate": 1, "next_bias": 1, "next_acc": 1}


def last_pair(g, h):
    return divmod(2 * g + h - 1, 2)


class SharedBanks:

    def __init__(self, ready, done):
        self.ready, self.done = Count(ready, USES_OF), done
        self.skipped = self.ready.total[0] % 2
        assert self.ready.total[1] % 2 == 0

    def number(self, t, step, j):
        return self.ready.steps_before(t, step) + j + (self.skipped if t is None else 0)

    def bank(self, t, step, j=0):
        return self.number(t, step, j) % 2

    def wait_product(self, eng, t, step, j=0):
        self.ready.wait(eng, t, step, j + 1)

    def taken(self, t, step, j=0):
        n = self.number(t, step, j) // 2 + 1
        if t is not None:
            n = t * (self.ready.total[1] // 2) + ((self.ready.total[0] + self.skipped) // 2 + n)
        return self.bank(t, step, j), n

    def wait_taken(self, eng, t, *uses, free=None):
        last = {}
        numbers = [(self.number(t, step, j), step, j, 0) for step, j in uses]
        if free is not None:
            numbers.append((self.number(t, *free) - 2, *free, 1))
        for number, step, j, earlier in sorted(numbers, key=lambda x: x[0]):
            last[number % 2] = (step, j, earlier)
        for step, j, earlier in last.values():
            bank, n = self.taken(t, step, j)
            n = n - earlier
            if t is not None or n > 0:
                eng.wait_ge(self.done[bank], n)


def retention_moe(nc, x, small, layer_w, w1, w3, w2, b2, select_c, out):
    where, n_small = columns(SMALL)
    where_w, n_layer = columns(LAYER_W)
    x_v = x.rearrange("a (m i p) d -> (a m) p i d", i=NT, p=P)
    out_v = out.rearrange("a (m i p) d -> (a m) p i d", i=NT, p=P)

    with ExitStack() as ctx:
        def sb(name, shape, dtype=F32):
            return ctx.enter_context(nc.sbuf_tensor(name, shape, dtype))

        def psum(name, shape):
            return ctx.enter_context(nc.psum_tensor(name, shape, F32))

        def sem(name):
            return ctx.enter_context(nc.semaphore(name))

        small_s = sb("small_s", [P, n_small])
        layer_s = sb("layer_s", [P, LAYERS, n_layer])
        up_hi = sb("up_hi", [P, 2, UNITS, KB * P], F32R)
        up_lo = sb("up_lo", [P, 2, UNITS, KB * P], F32R)
        w2_s = sb("w2_s", [P, UNITS, KB, P])
        b2_s = sb("b2_s", [EXPERTS, P])
        minus_half = sb("minus_half", [P, NT])
        out_bias = sb("out_bias", [P, P])
        pool_carrier = sb("pool_carrier", [P, 3 * len(STEPS)])
        dve_carrier = sb("dve_carrier", [P, len(STEPS)])

        x_in = sb("x_in", [P, NT, P])
        xn_next = sb("xn_next", [P, NT, P])
        xnT_next = sb("xnT_next", [P, MT])
        cw_next = sb("cw_next", [P, NT, EXPERTS])
        cwT_next = sb("cwT_next", [EXPERTS, MT])
        acc_next = sb("acc_next", [P, NT, P])
        stats_next = sb("stats_next", [P, NT, 6])
        mean_var_next = sb("mean_var_next", [P, NT, 2])
        var_eps_next = sb("var_eps_next", [P, NT])
        rstd_next = sb("rstd_next", [P, NT])
        logits = sb("logits", [P, NT, EXPERTS])
        top = sb("top", [P, NT])
        shifted = sb("shifted", [P, NT, EXPERTS])
        exps = sb("exps", [P, NT, EXPERTS])
        above = sb("above", [P, NT, EXPERTS, EXPERTS])
        ties = sb("ties", [P, NT, EXPERTS, EXPERTS])
        rank = sb("rank", [P, NT, EXPERTS])
        chosen = sb("chosen", [P, NT, EXPERTS])
        exps_sum = sb("exps_sum", [P, NT])
        chosen_sum = sb("chosen_sum", [P, NT])
        scale = sb("scale", [P, NT])

        res = sb("res", [P, NT, P])
        xnT_hi = sb("xnT_hi", [P, MT], F32R)
        xnT_lo = sb("xnT_lo", [P, MT], F32R)
        cw = sb("cw", [P, NT, EXPERTS])
        acc = sb("acc", [P, NT, P])
        stats = sb("stats", [P, NT, 6])
        mean_var = sb("mean_var", [P, NT, 2])
        var_eps = sb("var_eps", [P, NT])
        rstd = sb("rstd", [P, NT])
        normed = sb("normed", [P, NT, P])
        hT = sb("hT", [P, MT])
        qT = sb("qT", [P, NT, P])
        q_hi, q_lo, k_hi, k_lo = [sb(n, [P, MT], F32R) for n in ("q_hi", "q_lo", "k_hi", "k_lo")]
        select = sb("select", [P, 4, GROUPS, P], F32R)
        k_stack = sb("k_stack", [P, GROUPS, MT], F32R)
        q_stack = sb("q_stack", [P, GROUPS, NT, GH, P], F32R)
        kT = sb("kT", [P, NT, P])
        k_tok = sb("k_tok", [P, NT, P])
        v_tok = sb("v_tok", [P, NT, P])
        v_heads = sb("v_heads", [P, NT, GROUPS, GH * GP])
        gateT = sb("gateT", [P, MT])
        retT = sb("retT", [P, MT])
        scores = sb("scores", [P, 2, GH, P])
        chunk_kv = sb("chunk_kv", [P, NT, P])
        state = sb("state", [P, LAYERS, NT, P])
        gelus = sb("gelus", [P, FFN, MT])
        silus = sb("silus", [P, 2, MT])
        hidden = sb("hidden", [P, 2, KB, MT])
        out_s = sb("out_s", [P, NT, P])

        shared_p = psum("shared_p", [P, 2, MT])
        scores_p = psum("scores_p", [P, 2, MT])
        ret_p = psum("ret_p", [P, MT])
        up_p = psum("up_p", [P, 2, MT])
        down_p = psum("down_p", [P, MT])

        def col(name, l=None):
            a, b = where[name if l is None else f"{name}_{l}"]
            return small_s[:, a:b]

        def over(ap, n=NT):
            return ap.unsqueeze(1).broadcast_to([P, n, ap.shape[-1]])

        up_landed = [(gelus[:].rearrange("p a n -> p (a n)"), (0, slice(0, EXPERTS))),
                     (hidden[:].rearrange("p a k n -> p (a k n)"), (1, slice(0, EXPERTS))),
                     (scores[:].rearrange("p a j n -> p (a j n)")[:, 0:2 * P * KB], (0, slice(EXPERTS, UNITS))),
                     (scores[:].rearrange("p a j n -> p (a j n)")[:, 2 * P * KB:], (1, slice(EXPERTS, UNITS)))]

        select_landed = [retT[:]] + [b[:].rearrange("p i n -> p (i n)") for b in (k_tok, chunk_kv, acc)]

        def up_part(parts, where):
            n, units = where
            return parts[:, n, units].rearrange("p u c -> p (u c)")

        def weight(name, l):
            a, b = where_w[name]
            return layer_s[:, l, a:b]

        def tiles(ap):
            return ap.rearrange("p (i n) -> p i n", i=NT)

        def tile_of(ap, i):
            return ap[:, i * P:(i + 1) * P]

        s_small, s_layer, s_w2, s_b2 = [sem(f"{n}_loaded") for n in ("small", "layer_w", "w2", "b2")]
        s_up = [sem(f"up_piece_{n}_loaded") for n in range(4)]
        s_x = sem("x_loaded")
        s_select_loaded = sem("select_loaded")
        s_select = sem("select_ready")
        s_up_hi = sem("up_hi_ready")
        s_up_lo = sem("up_lo_ready")
        s_filled = sem("constants_filled")
        s_out_bias = sem("out_bias_ready")
        s_stored = sem("out_stored")

        x_biased_ready = Count(sem("x_biased_ready"), {"next_norm": 1})
        var_next_ready = Count(sem("var_next_ready"), {"next_norm": 1})
        rstd_next_ready = Count(sem("rstd_next_ready"), {"next_norm": 1})
        xn_next_ready = Count(sem("xn_next_ready"), {"next_norm": 1})
        shifted_ready = Count(sem("shifted_ready"), {"next_gate": 1})
        exps_ready = Count(sem("exps_ready"), {"next_gate": 1})
        cw_next_ready = Count(sem("cw_next_ready"), {"next_gate": 1})
        begun = Count(sem("begin_copies"), {"begin": 2})
        xnT_ready = Count(sem("xnT_ready"), {"begin": 1})
        var_ready = Count(sem("var_ready"), {"norm": 1})
        rstd_ready = Count(sem("rstd_ready"), {"norm": 1})
        normed_ready = Count(sem("normed_ready"), {"norm": 1})
        res_biased = Count(sem("res_biased"), {"norm": 1, ("norm", 0, 1): 0})
        hi_ready = Count(sem("k_and_q_hi_ready"), {"project": 2})
        k_lo_ready = Count(sem("k_lo_ready"), {"project": 1})
        q_lo_ready = Count(sem("q_lo_ready"), {"project": 1})
        xn_lo_ready = Count(sem("xn_lo_ready"), {"begin": 1})
        v_heads_ready = Count(sem("v_heads_ready"), {"project": 1})
        state_ready = Count(sem("state_ready"), {"state": NT - 1, "inter": 1}, credit=1)
        scored = Count(sem("scores_in_psum"), {"score": 2})
        masked = Count(sem("scores_masked"), {"score": 2})
        scores_used = Count(sem("scores_used"), {"pv": 2})
        retained = Count(sem("retention_in_psum"), {"inter": 1})
        gated = Count(sem("retention_gated"), {"inter": 1})
        w1_ready = Count(sem("w1_product"), {"moe": 1})
        w3_ready = Count(sem("w3_product"), {"moe": 1})
        silu_ready = Count(sem("silu_ready"), {"moe": 1}, credit=1)
        hidden_ready = Count(sem("hidden_ready"), {"moe": 1}, credit=2)
        down_steps = {("moe", u, 0): 1 for u in range(1, UNITS)} | {("moe_end",): 1}
        down_ready = Count(sem("down_product"), down_steps, credit=1)
        acc_updated = Count(sem("acc_updated"), down_steps, credit=1)
        out_ready = Count(sem("out_ready"), {"finish": 1})
        dve_link = Count(sem("vector_link"), {"norm": 2, "next_norm": 2, "next_gate": 9})
        shared = SharedBanks(sem("shared_product"), [sem("shared_taken_0"), sem("shared_taken_1")])

        def run(eng, step_of, weights_parts=lambda: None):
            for step in NEXT:
                step_of(None, step)
            weights_parts()
            with eng.Fori(0, MACROS - 1) as t:
                for step in STEPS:
                    step_of(t, step)
            for step in LAST_STEPS:
                step_of(MACROS - 1, step)

        block = ctx.enter_context(nc.Block())

        @block.sync
        def _(sp):
            sp.dma_start(x_in[:], x_v[0, :, :, :]).then_inc(s_x, 16)
            sp.dma_start(layer_s[:], layer_w).then_inc(s_layer, 16)
            for piece, (to, (n, units)) in enumerate(up_landed):
                sp.dma_start(to, (w1, w3)[n][:, units, :].rearrange("p u c -> p (u c)")).then_inc(s_up[piece], 16)
            sp.dma_start(w2_s[:], w2).then_inc(s_w2, 16)

            def step_of(t, step):
                if step[0] == "load" and t is not None:
                    xn_next_ready.wait_all_before(sp, t, step)
                    x_biased_ready.wait_all_before(sp, t, step)
                    sp.dma_start(x_in[:], x_v[t + 1, :, :, :]).then_inc(s_x, 16)
                if step[0] == "finish":
                    out_ready.wait(sp, t, step, 1)
                    sp.dma_start(out_v[t, :, :, :], out_s[:]).then_inc(s_stored, 16)

            run(sp, step_of)
            sp.wait_ge(s_stored, 16 * (MACROS + 1))

        @block.gpsimd
        def _(pool):
            pool.memset(minus_half[:], -0.5).then_inc(s_filled, 1)
            pool.memset(state[:], 0.0).then_inc(state_ready.sem, 1)
            pool.memset(v_heads[:], 0.0).then_inc(s_filled, 1)
            pool.wait_ge(s_small, 16)
            pool.tensor_tensor(out_bias[:], col("lnf_b"), col("sb2"), ALU.add).then_inc(s_out_bias, 1)
            pool.wait_ge(s_filled, 2)
            pool.wait_ge(s_out_bias, 1)

            def carry_wait(step, n=0):
                c = 3 * STEPS.index(step) + n
                pool.tensor_tensor(pool_carrier[:, c:c + 1], minus_half[:, 0:1], minus_half[:, 0:1], ALU.mult)

            def inverse_std(var_eps, done, to):
                pool.tensor_tensor(to[:], var_eps[:], minus_half[:], ALU.pow).then_inc(done.sem, 1)

            def step_of(t, step):
                kind = step[0]
                if kind == "begin":
                    normed_ready.wait_all_before(pool, t, step)
                    pool.tensor_tensor(res[:], xn_next[:], over(col("reto_b", 0)), ALU.add).then_inc(begun.sem, 1)
                    acc_updated.wait_all_before(pool, t, step)
                    carry_wait(step)
                    pool.tensor_copy(cw[:], cw_next[:]).then_inc(begun.sem, 1)
                elif kind == "next_norm":
                    pool.wait_ge(s_x, 16 if t is None else t * 16 + 32)
                    if t is not None:
                        acc_updated.wait(pool, t, ("moe", 1, 0), 1)
                    pool.tensor_tensor(acc_next[:], x_in[:], over(out_bias[:]), ALU.add).then_inc(x_biased_ready.sem, 1)
                    var_next_ready.wait(pool, t, step, 1)
                    inverse_std(var_eps_next, rstd_next_ready, rstd_next)
                elif kind == "norm":
                    l, w = step[1:]
                    var_ready.wait(pool, t, step, 1)
                    inverse_std(var_eps, rstd_ready, rstd)
                    normed_ready.wait(pool, t, step, 1)
                    if w == 3:
                        pool.tensor_tensor(out_s[:], out_s[:], over(col("lnf_g")), ALU.mult).then_inc(res_biased.sem, 1)
                    elif (l, w) != (0, 1):
                        bias = col("reto_b" if w == 1 else "ffn2_b", l)
                        pool.tensor_tensor(res[:], res[:], over(bias), ALU.add).then_inc(res_biased.sem, 1)
                elif kind == "project":
                    l = step[1]
                    hi_ready.wait(pool, t, step, 1)
                    pool.tensor_tensor(k_lo[:], kT[:].rearrange("p i n -> p (i n)"), k_hi[:].bitcast(F32),
                                       ALU.subtract).then_inc(k_lo_ready.sem, 1)
                    shared.wait_taken(pool, t, (step, 3))
                    carry_wait(step)
                    for i in range(NT):
                        own = v_heads[:, i].rearrange("p g (b e) -> p g b e", e=HD)[:, :, 0:GH * GH:GH + 1, :]
                        ins = pool.tensor_copy(own, v_tok[:, i].rearrange("p (g j e) -> p g j e", g=GROUPS, e=HD))
                    ins.then_inc(v_heads_ready.sem, 1)

            run(pool, step_of)

        @block.scalar
        def _(act):
            act.dma_start(small_s[:], small).then_inc(s_small, 16)
            for part, landed in enumerate(select_landed):
                act.dma_start(landed, select_c[:, part, :]).then_inc(s_select_loaded, 16)
            act.dma_start(b2_s[:], b2).then_inc(s_b2, 16)
            act.wait_ge(s_small, 16)
            act.activation(silus[:, 0, 0:1], col("ident")[:, 0:1], ACT.Silu).then_inc(silu_ready.sem, 1)

            def take(t, step, j, to, func=ACT.Copy, **more):
                shared.wait_product(act, t, step, j)
                bank = shared.bank(t, step, j)
                return act.activation(to, shared_p[0:to.shape[0], bank, :], func, **more).then_inc(shared.done[bank], 1)

            def step_of(t, step):
                kind = step[0]
                if kind == "begin":
                    down_ready.wait_all_before(act, t, step)
                    act.activation(xnT_hi[:], xnT_next[:], ACT.Copy).then_inc(xnT_ready.sem, 1)
                elif kind == "next_turn":
                    if t is not None:
                        xnT_ready.wait_all_before(act, t, step)
                    take(t, step, 0, xnT_next[:])
                elif kind == "next_gate":
                    shifted_ready.wait(act, t, step, 1)
                    act.activation(exps[:], shifted[:], ACT.Exp).then_inc(exps_ready.sem, 1)
                elif kind == "next_bias":
                    take(t, step, 0, cwT_next[:])
                elif kind == "turn":
                    l, w = step[1:]
                    take(t, step, 0, hT[:], ACT.Identity, scale=col(f"ln{w}_g", l), bias=col(f"ln{w}_b", l))
                elif kind == "project":
                    for n, (whole, hi) in enumerate(((kT, k_hi), (qT, q_hi))):
                        shared.wait_taken(act, t, (step, n))
                        act.activation(hi[:], whole[:].rearrange("p i n -> p (i n)"), ACT.Copy).then_inc(hi_ready.sem, 1)
                    take(t, step, 2, gateT[:], ACT.Silu, bias=col("bx", step[1]))
                elif kind == "stack":
                    g = step[2]
                    take(t, step, 0, k_stack[:, g, :])
                    shared.wait_product(act, t, step, 1)
                    for j in range(GH):
                        ins = act.activation(q_stack[:, g, :, j, :], tiles(shared_p[:, shared.bank(t, step, 1), :]), ACT.Copy,
                                             scale=col("head_mask")[:, j:j + 1])
                    ins.then_inc(shared.done[shared.bank(t, step, 1)], 1)
                elif kind == "turn_k":
                    take(t, step, 0, k_tok[:].rearrange("p i n -> p (i n)"))
                elif kind == "ffn1":
                    for f in range(FFN):
                        take(t, step, f, gelus[:, f, :], ACT.Gelu, bias=col("ffn1_b", step[1])[:, f:f + 1])
                elif kind == "moe":
                    u, k = step[1:]
                    w1_ready.wait(act, t, step, 1)
                    hidden_ready.wait(act, t, step, -1)
                    act.activation(silus[:, k, :], up_p[:, 0, :], ACT.Silu,
                                   bias=col("b1")[:, u * KB + k:u * KB + k + 1]).then_inc(silu_ready.sem, 1)

            def weights_parts():
                act.wait_ge(s_select_loaded, 4 * 16)
                for part, landed in enumerate(select_landed):
                    ins = act.activation(select[:, part].rearrange("p g n -> p (g n)"), landed, ACT.Copy)
                ins.then_inc(s_select, 1)
                for n, (landed, where) in enumerate(up_landed):
                    act.wait_ge(s_up[n], 16)
                    act.activation(up_part(up_hi, where), landed, ACT.Copy).then_inc(s_up_hi, 1)

            run(act, step_of, weights_parts)

        @block.vector
        def _(dve):
            dve.memset(stats[:], 0.0).then_inc(hidden_ready.sem, 2)
            dve.memset(mean_var[:], 0.0).then_inc(acc_updated.sem, 1)
            dve.memset(rank[:], 0.0).then_inc(s_stored, 16)
            dve.memset(exps_sum[:], 0.0).then_inc(shared.done[0], shared.skipped)
            dve.wait_ge(s_small, 16)
            linked = [None, 0]

            def link(t, step, ins):
                if linked[0] != (phase_of(t), step):
                    linked[:] = [(phase_of(t), step), 0]
                linked[1] += 1
                ins.then_inc(dve_link.sem, 1)
                dve_link.wait(dve, t, step, linked[1])

            def normalise(t, step, rows, stats, mean_var, var_eps, rstd, to, var_done, rstd_done, done):
                for i in range(NT):
                    ins = dve.bn_stats(stats[:, i, :], rows[:, i, :])
                link(t, step, ins)
                c = STEPS.index(step)
                dve.memset(dve_carrier[:, c:c + 1], 0.0)
                for i in range(NT):
                    ins = dve.bn_aggr(mean_var[:, i, :], stats[:, i, :])
                link(t, step, ins)
                dve.tensor_scalar(var_eps[:], mean_var[:, :, 1], EPS, None, ALU.add).then_inc(var_done.sem, 1)
                rstd_done.wait(dve, t, step, 1)
                for i in range(NT):
                    ins = dve.tensor_scalar(to[:, i, :], rows[:, i, :], mean_var[:, i, 0:1], rstd[:, i:i + 1],
                                            ALU.subtract, ALU.mult)
                ins.then_inc(done.sem, 1)

            def product(t, step, j=0):
                shared.wait_product(dve, t, step, j)
                return shared_p[:, shared.bank(t, step, j), :]

            def taken(t, step, j, ins):
                ins.then_inc(shared.done[shared.bank(t, step, j)], 1)

            def gate(t, step):
                p = product(t, step)[:, 0:NT * EXPERTS].rearrange("p (i e) -> p i e", e=EXPERTS)
                if t is not None:
                    begun.wait_all_before(dve, t, step)
                taken(t, step, 0, dve.tensor_tensor(logits[:], p, over(col("gate_b")), ALU.add))
                shared.wait_taken(dve, t, (step, 0))
                mine = logits[:].unsqueeze(3).broadcast_to([P, NT, EXPERTS, EXPERTS])
                other = logits[:].unsqueeze(2).broadcast_to([P, NT, EXPERTS, EXPERTS])
                link(t, step, dve.tensor_reduce(top[:], logits[:], AX_X, ALU.max))
                dve.tensor_tensor(shifted[:], logits[:], top[:].unsqueeze(2).broadcast_to([P, NT, EXPERTS]),
                                  ALU.subtract).then_inc(shifted_ready.sem, 1)
                dve.tensor_tensor(above[:], other, mine, ALU.is_gt)
                link(t, step, dve.tensor_tensor(ties[:], other, mine, ALU.is_equal))
                flat = "p i a b -> p i (a b)"
                link(t, step, dve.tensor_tensor(ties[:].rearrange(flat), ties[:].rearrange(flat), over(col("before")), ALU.mult))
                link(t, step, dve.tensor_tensor(above[:], above[:], ties[:], ALU.add))
                link(t, step, dve.tensor_reduce(rank[:], above[:], AX_X, ALU.add))
                exps_ready.wait(dve, t, step, 1)
                dve.tensor_reduce(exps_sum[:], exps[:], AX_X, ALU.add)
                link(t, step, dve.scalar_tensor_tensor(out=chosen[:], in0=rank[:], scalar=1.5, in1=exps[:],
                                                       op0=ALU.is_lt, op1=ALU.mult))
                link(t, step, dve.tensor_reduce(chosen_sum[:], chosen[:], AX_X, ALU.add))
                link(t, step, dve.scalar_tensor_tensor(out=chosen_sum[:], in0=exps_sum[:], scalar=1e-20, in1=chosen_sum[:],
                                                       op0=ALU.mult, op1=ALU.add))
                link(t, step, dve.reciprocal(scale[:], chosen_sum[:]))
                dve.tensor_tensor(cw_next[:], chosen[:], scale[:].unsqueeze(2).broadcast_to([P, NT, EXPERTS]),
                                  ALU.mult).then_inc(cw_next_ready.sem, 1)

            def add_to_acc(t, step, u):
                down_ready.wait(dve, t, step, 1)
                acc_updated.wait(dve, t, step, 0)
                sums = acc
                if u == 0:
                    begun.wait(dve, t, ("begin",), 2)
                    shared.wait_taken(dve, t, (("made", "next_acc"), 0))
                    sums = acc_next
                if u < EXPERTS:
                    for i in range(NT):
                        ins = dve.scalar_tensor_tensor(out=acc[:, i, :], in0=tile_of(down_p, i), scalar=cw[:, i, u:u + 1],
                                                       in1=sums[:, i, :], op0=ALU.mult, op1=ALU.add)
                else:
                    ins = dve.tensor_tensor(acc[:], tiles(down_p[:]), acc[:], ALU.add)
                ins.then_inc(acc_updated.sem, 1)

            def step_of(t, step):
                kind = step[0]
                if kind == "begin":
                    xnT_ready.wait(dve, t, step, 1)
                    dve.tensor_tensor(xnT_lo[:], xnT_next[:], xnT_hi[:].bitcast(F32), ALU.subtract).then_inc(xn_lo_ready.sem, 1)
                elif kind == "next_norm":
                    dve.wait_ge(s_x, 16 if t is None else t * 16 + 32)
                    if t is not None:
                        begun.wait(dve, t, ("begin",), 1)
                    normalise(t, step, x_in, stats_next, mean_var_next, var_eps_next, rstd_next, xn_next,
                              var_next_ready, rstd_next_ready, xn_next_ready)
                elif kind == "next_gate":
                    gate(t, step)
                elif kind == "next_acc":
                    x_biased_ready.wait(dve, t, ("next_norm",), 1)
                    taken(t, step, 0, dve.tensor_tensor(acc_next[:], tiles(product(t, step)), acc_next[:], ALU.add))
                elif kind == "norm":
                    l, w = step[1:]
                    if (l, w) == (0, 1):
                        xn_next_ready.wait(dve, t, ("next_norm",), 1)
                        if t is not None:
                            shared.wait_product(dve, t, ("turn", LAYERS - 1, 2))
                    else:
                        shared.wait_taken(dve, t, (("reto", l) if w == 2 else ("ffn2", l - 1 if w == 1 else l), 0))
                    if w == 3:
                        dve.wait_ge(s_stored, t * 16 + 16)
                    normalise(t, step, xn_next if (l, w) == (0, 1) else res, stats, mean_var, var_eps, rstd,
                              out_s if w == 3 else normed, var_ready, rstd_ready, normed_ready)
                elif kind == "project":
                    l = step[1]
                    for j, (to, bias, decay) in enumerate(((kT, "bk", "decay_k"), (qT, "bq", "decay_q"))):
                        taken(t, step, j, dve.scalar_tensor_tensor(out=to[:], in0=tiles(product(t, step, j)), scalar=col(bias, l),
                                                                   in1=over(col(decay)), op0=ALU.add, op1=ALU.mult))
                    hi_ready.wait(dve, t, step, 2)
                    dve.tensor_tensor(q_lo[:], qT[:].rearrange("p i n -> p (i n)"), q_hi[:].bitcast(F32),
                                      ALU.subtract).then_inc(q_lo_ready.sem, 1)
                    taken(t, step, 3, dve.tensor_tensor(v_tok[:], tiles(product(t, step, 3)), over(col("bv", l)), ALU.add))
                elif kind == "state":
                    l = step[1]
                    taken(t, step, 0, dve.scalar_tensor_tensor(out=chunk_kv[:], in0=tiles(product(t, step)), scalar=col("decay_chunk"),
                                                               in1=over(col("same_head")), op0=ALU.mult, op1=ALU.mult))
                    shared.wait_taken(dve, t, (step, 0))
                    for i in range(NT - 1):
                        state_ready.wait(dve, t, step, i)
                        next_state(l, i)
                elif kind == "score":
                    for n in range(2):
                        if step[2:] != (0, 0):
                            scores_used.wait(dve, t, ("pv", step[1], *last_pair(*step[2:])), n + 1)
                        scored.wait(dve, t, step, n + 1)
                        dve.tensor_tensor(scores[:, n], scores_p[:, n, :].rearrange("p (j n) -> p j n", j=GH),
                                          over(col("causal"), GH), ALU.mult).then_inc(masked.sem, 1)
                elif kind == "inter":
                    l = step[1]
                    retained.wait(dve, t, step, 1)
                    shared.wait_taken(dve, t, (projected(l), 2))
                    dve.tensor_tensor(retT[:], ret_p[:], gateT[:], ALU.mult).then_inc(gated.sem, 1)
                    state_ready.wait(dve, t, step, 0)
                    next_state(l, NT - 1)
                elif kind in ("reto", "ffn2"):
                    l = step[1]
                    if (kind, l) == ("reto", 0):
                        begun.wait(dve, t, ("begin",), 1)
                    else:
                        res_biased.wait(dve, t, ("norm", l, 1 if kind == "reto" else 2), 1)
                    taken(t, step, 0, dve.tensor_tensor(res[:], tiles(product(t, step)), res[:], ALU.add))
                elif kind == "moe":
                    u, k = step[1:]
                    silu_ready.wait(dve, t, step, 1)
                    w3_ready.wait(dve, t, step, 1)
                    b = u * KB + k
                    dve.scalar_tensor_tensor(out=hidden[:, u % 2, k, :], in0=up_p[:, 1, :], scalar=col("b3")[:, b:b + 1],
                                             in1=silus[:, k, :], op0=ALU.add, op1=ALU.mult).then_inc(hidden_ready.sem, 1)
                    if k == 0 and u > 0:
                        add_to_acc(t, step, u - 1)
                elif kind == "moe_end":
                    add_to_acc(t, step, UNITS - 1)
                elif kind == "finish":
                    res_biased.wait(dve, t, ("norm", LAYERS - 1, 3), 1)
                    acc_updated.wait(dve, t, ("moe_end",), 1)
                    dve.tensor_tensor(out_s[:], out_s[:], acc[:], ALU.add).then_inc(out_ready.sem, 1)

            def next_state(l, i):
                dve.scalar_tensor_tensor(out=state[:, l, (i + 1) % NT], in0=state[:, l, i], scalar=col("decay_chunk"),
                                         in1=chunk_kv[:, i], op0=ALU.mult, op1=ALU.add).then_inc(state_ready.sem, 1)

            def weights_parts():
                dve.wait_ge(s_select, 1)
                for n, (landed, where) in enumerate(up_landed):
                    dve.wait_ge(s_up_hi, n + 1)
                    dve.tensor_tensor(up_part(up_lo, where), landed, up_part(up_hi, where).bitcast(F32), ALU.subtract).then_inc(s_up_lo, 1)

            run(dve, step_of, weights_parts)

        @block.tensor
        def _(pe):
            pe.wait_ge(s_small, 16)
            shared_ready = shared.ready.sem

            def use(t, step, j=0, of=()):
                shared.wait_taken(pe, t, *of, free=(step, j))
                return shared_p[:, shared.bank(t, step, j), :]

            def turn(to, rows):
                for i in range(NT):
                    ins = pe.transpose(tile_of(to, i)[0:rows.shape[2], :], rows[:, i, :], col("ident"))
                ins.then_inc(shared_ready, 1)

            def tokens_product(to, lhs, rhs):
                n = rhs[0].shape[-1]
                for i in range(NT):
                    for b, (left, right) in enumerate(zip(lhs, rhs)):
                        ins = pe.matmul(to[:, i * n:(i + 1) * n], tile_of(left, i), right,
                                        start=(b == 0), stop=(b == len(rhs) - 1))
                return ins

            def step_of(t, step):
                kind = step[0]
                if kind == "next_turn":
                    xn_next_ready.wait(pe, t, ("next_norm",), 1)
                    turn(use(t, step), xn_next)
                elif kind == "next_gate":
                    to = use(t, step, of=[(("next_turn",), 0)])
                    tokens_product(to, [xnT_next], [col("gate_w")]).then_inc(shared_ready, 1)
                elif kind == "next_bias":
                    cw_next_ready.wait(pe, t, ("next_gate",), 1)
                    turn(use(t, step), cw_next)
                elif kind == "next_acc":
                    to = use(t, step, of=[(("next_bias",), 0)])
                    pe.wait_ge(s_b2, 16)
                    tokens_product(to, [cwT_next], [b2_s[:]]).then_inc(shared_ready, 1)
                    if t is None:
                        pe.transpose(down_p[:, 0:P], col("ident"), col("ident")).then_inc(down_ready.sem, 1)
                elif kind == "turn":
                    normed_ready.wait(pe, t, ("norm", *step[1:]), 1)
                    turn(use(t, step), normed)
                elif kind == "project":
                    l = step[1]
                    pe.wait_ge(s_layer, 16)
                    for j, block_of in enumerate((1, 0, 3)):
                        to = use(t, step, j, of=[(("turn", l, 1), 0)])
                        pe.matmul(to, tile_of(weight("proj", l), block_of), hT[:], start=True, stop=True).then_inc(shared_ready, 1)
                    tokens_product(use(t, step, 3), [hT], [tile_of(weight("proj", l), 2)]).then_inc(shared_ready, 1)
                elif kind == "stack":
                    l, g = step[1:]
                    pe.wait_ge(s_select, 1)
                    for j, (hi, lo) in enumerate(((k_hi, k_lo), (q_hi, q_lo))):
                        if g == 0:
                            (k_lo_ready, q_lo_ready)[j].wait(pe, t, projected(l), 1)
                        to = use(t, step, j)
                        pe.matmul(to, select[:, 2 * j, g], hi[:], start=True, stop=False)
                        pe.matmul(to, select[:, 2 * j + 1, g], lo[:], start=False, stop=True).then_inc(shared_ready, 1)
                elif kind == "turn_k":
                    turn(use(t, step, of=[(projected(step[1]), 0)]), kT)
                elif kind == "state":
                    l = step[1]
                    to = use(t, step, of=[(("turn_k", l), 0), (projected(l), 3)])
                    for i in range(NT):
                        ins = pe.matmul(tile_of(to, i), k_tok[:, i], v_tok[:, i], start=True, stop=True)
                    ins.then_inc(shared_ready, 1)
                elif kind == "score":
                    l, g, h = step[1:]
                    if h == 0:
                        shared.wait_taken(pe, t, (("stack", l, g), 0), (("stack", l, g), 1))
                    for n in range(2):
                        if (g, h) != (0, 0):
                            masked.wait(pe, t, ("score", l, *last_pair(g, h)), n + 1)
                        i = 2 * h + n
                        pe.matmul(scores_p[:, n, :], tile_of(k_stack[:, g], i), q_stack[:, g, i].rearrange("p j n -> p (j n)"),
                                  start=True, stop=True).then_inc(scored.sem, 1)
                elif kind == "pv":
                    l, g, h = step[1:]
                    if (g, h) == (0, 0):
                        v_heads_ready.wait(pe, t, projected(l), 1)
                    for n in range(2):
                        i = 2 * h + n
                        masked.wait(pe, t, ("score", *step[1:]), n + 1)
                        for j in range(GH):
                            ins = pe.matmul(ret_p[g * GP:(g + 1) * GP, i * P:(i + 1) * P], v_heads[:, i, g, j * GP:(j + 1) * GP],
                                            scores[:, n, j, :], start=(i == 0 and j == 0), stop=True, skip_group_check=True)
                        ins.then_inc(scores_used.sem, 1)
                elif kind == "inter":
                    l = step[1]
                    for i in range(NT):
                        if i < 2:
                            state_ready.wait(pe, t, ("state", l), i * (NT - 1))
                        ins = pe.matmul(tile_of(ret_p, i), state[:, l, i], qT[:, i], start=False, stop=True, skip_group_check=True)
                    ins.then_inc(retained.sem, 1)
                elif kind == "reto":
                    gated.wait(pe, t, ("inter", step[1]), 1)
                    tokens_product(use(t, step), [retT], [weight("reto", step[1])]).then_inc(shared_ready, 1)
                elif kind == "ffn1":
                    l = step[1]
                    for f in range(FFN):
                        to = use(t, step, f, of=[(("turn", l, 2), 0)])
                        pe.matmul(to, tile_of(weight("ffn1", l), f), hT[:], start=True, stop=True).then_inc(shared_ready, 1)
                elif kind == "ffn2":
                    l = step[1]
                    to = use(t, step, of=[(("ffn1", l), f) for f in range(FFN)])
                    tokens_product(to, [gelus[:, f, :] for f in range(FFN)],
                                   [tile_of(weight("ffn2", l), f) for f in range(FFN)]).then_inc(shared_ready, 1)
                elif kind == "moe":
                    u, k = step[1:]
                    if (u, k) == (0, 0):
                        xn_lo_ready.wait(pe, t, ("begin",), 1)
                        pe.wait_ge(s_up_lo, 4)
                    silu_ready.wait(pe, t, step, 0)
                    up(0, u, k).then_inc(w1_ready.sem, 1)
                    hidden_ready.wait(pe, t, step, 0)
                    up(1, u, k).then_inc(w3_ready.sem, 1)
                    if k == 0 and u > 0:
                        down(t, step, u - 1)
                elif kind == "moe_end":
                    down(t, step, UNITS - 1)

            def up(n, u, k):
                parts = ((up_hi, xnT_hi), (up_hi, xnT_lo), (up_lo, xnT_hi))
                for b, (w, xt) in enumerate(parts):
                    ins = pe.matmul(up_p[:, n, :], tile_of(w[:, n, u], k), xt[:], start=(b == 0), stop=(b == len(parts) - 1))
                return ins

            def down(t, step, u):
                if u == 0:
                    pe.wait_ge(s_w2, 16)
                hidden_ready.wait(pe, t, ("moe", u, KB - 1), 1)
                acc_updated.wait(pe, t, step, 0)
                tokens_product(down_p, [hidden[:, u % 2, k] for k in range(KB)],
                               [w2_s[:, u, k] for k in range(KB)]).then_inc(down_ready.sem, 1)

            run(pe, step_of)


IN_NAMES = ["L0_attn_x", "small", "layer_w", "w1", "w3", "w2", "b2", "select"]


def decays():
    gamma = 1.0 - 2.0 ** (-5.0 - np.arange(HEADS))
    by_row = np.repeat(gamma, HD)[:, None]
    n = np.arange(P)[None, :]
    return (by_row ** n).astype(np.float32), (by_row ** -n).astype(np.float32), (by_row ** P).astype(np.float32)


def selections():
    s = np.zeros((P, 4, GROUPS, 4, GP), np.float32)
    for part, copies in enumerate(((0, 2), (1, 3), (0, 1), (2, 3))):
        for g in range(GROUPS):
            for c in copies:
                s[np.arange(GP) + g * GP, part, g, c, np.arange(GP)] = 1
    return s.reshape(P, 4, -1)


def laid_out(a):
    a = {name: np.asarray(value) for name, value in a.items()}
    rows = lambda v: np.broadcast_to(v.reshape(1, -1), (P, v.size))
    cols = lambda v: v.reshape(-1, P).T
    decay_q, decay_k, decay_chunk = decays()
    r = np.arange(P)
    e = np.arange(EXPERTS)
    f = {
        "ident": np.eye(P, dtype=np.float32),
        "causal": (r[None, :] >= r[:, None]).astype(np.float32),
        "decay_q": decay_q, "decay_k": decay_k, "decay_chunk": decay_chunk,
        "same_head": (r[None, :] // HD == r[:, None] // HD).astype(np.float32),
        "head_mask": ((r[:, None] // HD) % GH == np.arange(GH)[None, :]).astype(np.float32),
        "before": rows((e[None, :] < e[:, None]).astype(np.float32)),
        "gate_b": rows(a["L0_ffn_gate_b"]), "gate_w": a["L0_ffn_gate_w"].T,
        "b1": np.concatenate([cols(a["L0_ffn_b1"]), cols(a["L0_ffn_sb1"])], 1),
        "b3": np.concatenate([cols(a["L0_ffn_b3"]), cols(a["L0_ffn_sb3"])], 1),
        "lnf_g": rows(a["L0_attn_lnf_g"]), "lnf_b": rows(a["L0_attn_lnf_b"]), "sb2": rows(a["L0_ffn_sb2"]),
    }
    for l in range(LAYERS):
        bq, bk, bv, bx = a["L0_attn_proj_b"][l].reshape(4, P)
        f |= {f"ln1_g_{l}": cols(a["L0_attn_ln1_g"][l]), f"ln1_b_{l}": cols(a["L0_attn_ln1_b"][l]),
              f"ln2_g_{l}": cols(a["L0_attn_ln2_g"][l]), f"ln2_b_{l}": cols(a["L0_attn_ln2_b"][l]),
              f"bq_{l}": cols(bq), f"bk_{l}": cols(bk), f"bx_{l}": cols(bx), f"bv_{l}": rows(bv),
              f"ffn1_b_{l}": cols(a["L0_attn_ffn1_b"][l]), f"reto_b_{l}": rows(a["L0_attn_reto_b"][l]),
              f"ffn2_b_{l}": rows(a["L0_attn_ffn2_b"][l])}
    small = np.concatenate([f[name] for name, _ in SMALL], 1)
    by_in = lambda w: w.reshape(LAYERS, -1, P, w.shape[-1]).transpose(2, 0, 1, 3).reshape(P, LAYERS, -1)
    layer_w = np.concatenate([by_in(a[f"L0_attn_{n}_w"]) for n, _ in LAYER_W], 2)
    up = lambda w, sw: np.concatenate([w.transpose(2, 0, 1), sw.reshape(UNITS - EXPERTS, KB * P, P).transpose(2, 0, 1)], 1)
    w2, sw2 = a["L0_ffn_w2"], a["L0_ffn_sw2"]
    down = np.concatenate([w2.reshape(EXPERTS, P, KB, P).transpose(3, 0, 2, 1),
                           sw2.reshape(P, UNITS - EXPERTS, KB, P).transpose(3, 1, 2, 0)], 1)
    return {"L0_attn_x": a["L0_attn_x"], "small": small, "layer_w": layer_w, "w1": up(a["L0_ffn_w1"], a["L0_ffn_sw1"]),
            "w3": up(a["L0_ffn_w3"], a["L0_ffn_sw3"]), "w2": down, "b2": a["L0_ffn_b2"], "select": selections()}


def kernel(**inputs):
    import concourse.bacc as bacc
    from concourse.bass_utils import run_bass_kernel_spmd

    nc = bacc.Bacc("TRN2", target_bir_lowering=False, num_devices=1)
    arrays, args = {}, []
    placed = laid_out(inputs)
    for name in IN_NAMES:
        arrays[f"in_{name}"] = np.ascontiguousarray(placed[name])
        args.append(nc.dram_tensor(f"in_{name}", arrays[f"in_{name}"].shape, F32, kind="ExternalInput").ap())
    args.append(nc.dram_tensor("out", (1, N_TOK, P), F32, kind="ExternalOutput").ap())
    retention_moe(nc, *args)
    r = run_bass_kernel_spmd(nc, [arrays], core_ids=[0])
    return r.results[0]["out"]
```

```python
from contextlib import ExitStack

import numpy as np

import concourse.bass as bass
from concourse import mybir

F32 = mybir.dt.float32
F32R = mybir.dt.float32r
ALU = mybir.AluOpType
ACT = mybir.ActivationFunctionType
AX_X = mybir.AxisListType.X

P = 128
N_TOK = 2048
NT = 4
MT = NT * P
MACROS = N_TOK // MT
LAYERS = 2
HEADS = 16
HD = P // HEADS
GROUPS = 4
GH = HEADS // GROUPS
GP = P // GROUPS
FFN = 4
EXPERTS = 8
UNITS = EXPERTS + 2
KB = 2
EPS = 1e-5

PER_LAYER = [("ln1_g", 1), ("ln1_b", 1), ("ln2_g", 1), ("ln2_b", 1), ("bq", 1), ("bk", 1), ("bx", 1),
             ("ffn1_b", FFN), ("bv", P), ("reto_b", P), ("ffn2_b", P)]
SMALL = ([("ident", P), ("causal", P), ("decay_q", P), ("decay_k", P), ("same_head", P), ("decay_chunk", 1),
          ("head_mask", GH), ("before", EXPERTS * EXPERTS), ("gate_b", EXPERTS), ("gate_w", EXPERTS),
          ("b1", UNITS * KB), ("b3", UNITS * KB), ("lnf_g", P), ("lnf_b", P), ("sb2", P)]
         + [(f"{n}_{l}", w) for l in range(LAYERS) for n, w in PER_LAYER])
LAYER_W = [("k", P), ("qx", 2 * P), ("v", P), ("ffn1", FFN * P), ("reto", P), ("ffn2", FFN * P)]


def columns(fields):
    at, where = 0, {}
    for name, width in fields:
        where[name] = (at, at + width)
        at += width
    return where, at


MOE, DOWN = "moe", "down"


def numbered(steps):
    halves = iter([("moe", u, k) for u in range(UNITS) for k in range(KB)])
    downs = iter([("down", u) for u in range(UNITS)])
    return [next(halves) if step is MOE else next(downs) if step is DOWN else step for step in steps]


STEPS = numbered([
    ("begin",), ("stack", 0, 0), MOE, ("stack", 0, 1), ("load",), ("score", 0, 0, 0), ("turn_k", 0),
    ("pv", 0, 0, 0), ("score", 0, 0, 1), MOE, ("score", 0, 1, 0), ("stack", 0, 2), ("pv", 0, 0, 1),
    ("score", 0, 1, 1), ("state", 0), MOE, ("pv", 0, 1, 0), ("score", 0, 2, 0), ("stack", 0, 3), DOWN,
    ("pv", 0, 1, 1), ("pv", 0, 2, 0), ("score", 0, 2, 1), MOE, ("score", 0, 3, 0), ("pv", 0, 2, 1),
    ("pv", 0, 3, 0), ("score", 0, 3, 1), DOWN, MOE, ("pv", 0, 3, 1), ("inter", 0), MOE, ("reto", 0),
    ("norm", 0, 2), MOE, ("apply", 0, 2), DOWN, MOE, ("turn", 0, 2), MOE, ("ffn1", 0), ("next_norm",), DOWN, MOE,
    ("ffn2", 0), ("norm", 1, 1), MOE, ("next_turn",), ("apply", 1, 1), MOE, DOWN, ("turn", 1, 1), ("project", 1),
    ("next_gate",), ("next_choose",), ("stack", 1, 0), ("turn_k", 1), MOE, ("score", 1, 0, 0), ("stack", 1, 1),
    ("pv", 1, 0, 0), ("score", 1, 0, 1), DOWN, ("stack", 1, 2), ("score", 1, 1, 0), ("pv", 1, 0, 1),
    ("score", 1, 1, 1), ("state", 1), ("pv", 1, 1, 0), MOE, ("stack", 1, 3), ("score", 1, 2, 0), ("pv", 1, 1, 1),
    DOWN, MOE, ("pv", 1, 2, 0), ("score", 1, 2, 1), MOE, ("score", 1, 3, 0), ("pv", 1, 2, 1), ("score", 1, 3, 1),
    MOE, ("pv", 1, 3, 0), ("pv", 1, 3, 1), ("inter", 1), DOWN, ("reto", 1), ("norm", 1, 2), MOE, ("apply", 1, 2),
    ("next_bias",), MOE, DOWN, ("turn", 1, 2), ("norm", 0, 1), ("apply", 0, 1), MOE, ("ffn1", 1), ("turn", 0, 1),
    ("ffn2", 1), ("project", 0), ("norm", 1, 3), ("apply", 1, 3), ("next_acc",), ("next_parts",), DOWN,
    ("finish",)])
NEXT = [("load",), ("next_norm",), ("norm", 0, 1), ("apply", 0, 1), ("next_turn",), ("next_gate",), ("next_choose",),
        ("turn", 0, 1), ("next_bias",), ("project", 0), ("next_parts",), ("next_acc",)]


def moved(places):
    by = lambda step: places.get(step, 0)
    return sorted(STEPS, key=lambda step: STEPS.index(step) + by(step) + np.sign(by(step)) / 2)


ACT_STEPS = moved({("moe", 4, 0): 1, ("ffn1", 1): -1})
DVE_STEPS = moved({("turn", 0, 2): -2, ("moe", 6, 0): 1, ("moe", 7, 1): 1, ("moe", 0, 0): 3, ("next_norm",): -2,
                   ("apply", 1, 3): 2, ("moe", 1, 1): 1})


OWN_BANKS = {("moe", 3, 1), ("moe", 6, 0)}


def borrowed_banks():
    borrowing, before, last = set(), {}, {True: None, False: None}
    free = borrows = True
    for step in STEPS:
        if step[0] == "moe":
            borrows = free and not borrows and step not in OWN_BANKS
            if borrows:
                borrowing.add(step)
            before[step], last[borrows] = last[borrows], step
        elif step[0] == "score":
            if free:
                before[step], free, borrows = last[True], False, False
        elif step[0] == "inter":
            free = True
    return borrowing, before


BORROWING, BANKS_BEFORE = borrowed_banks()


def phases(steps):
    return NEXT, steps, [step for step in steps if step not in NEXT]


def phase_of(t):
    return 0 if t is None else 2 if isinstance(t, int) else 1


def projected(l):
    return ("project", l) if l > 0 else ("made", "project", l)


class Count:

    def __init__(self, sem, adds, credit=0, steps=STEPS):
        self.sem, self.adds, self.credit = sem, adds, credit
        self.before, self.total = [], []
        for steps in phases(steps):
            at, n = {}, 0
            for step in steps:
                at[step] = n
                n += self.of(step)
            self.before.append(at)
            self.total.append(n)

    def of(self, step):
        return self.adds.get(step, self.adds.get(step[0], 0))

    def steps_before(self, t, step):
        if step[0] != "made":
            return self.before[phase_of(t)][step]
        step = step[1:]
        left = self.total[1] - self.before[1][step]
        assert phase_of(t) > 0 and left == self.total[0] - self.before[0][step]
        return -left

    def value(self, t, step, n):
        phase = phase_of(t)
        n += self.steps_before(t, step) + self.credit
        return n if phase == 0 else t * self.total[1] + (self.total[0] + n)

    def wait(self, eng, t, step, n):
        eng.wait_ge(self.sem, self.value(t, step, n))

    def wait_all_before(self, eng, t, step):
        self.wait(eng, t, step, 0)


USES_OF = {"turn": 1, "project": 4, "stack": 2, "turn_k": 1, "state": 1, "reto": 1, "ffn1": FFN, "ffn2": 1,
           "next_turn": 1, "next_gate": 1, "next_bias": 1, "next_acc": 1}


def last_pair(g, h):
    return divmod(2 * g + h - 1, 2)


class SharedBanks:

    def __init__(self, ready, done):
        self.ready, self.done = Count(ready, USES_OF), done
        self.skipped = self.ready.total[0] % 2
        assert self.ready.total[1] % 2 == 0

    def number(self, t, step, j):
        return self.ready.steps_before(t, step) + j + (self.skipped if t is None else 0)

    def bank(self, t, step, j=0):
        return self.number(t, step, j) % 2

    def wait_product(self, eng, t, step, j=0):
        self.ready.wait(eng, t, step, j + 1)

    def taken(self, t, step, j=0):
        n = self.number(t, step, j) // 2 + 1
        if t is not None:
            n = t * (self.ready.total[1] // 2) + ((self.ready.total[0] + self.skipped) // 2 + n)
        return self.bank(t, step, j), n

    def wait_taken(self, eng, t, *uses, free=None):
        last = {}
        numbers = [(self.number(t, step, j), step, j, 0) for step, j in uses]
        if free is not None:
            numbers.append((self.number(t, *free) - 2, *free, 1))
        for number, step, j, earlier in sorted(numbers, key=lambda x: x[0]):
            last[number % 2] = (step, j, earlier)
        for step, j, earlier in last.values():
            bank, n = self.taken(t, step, j)
            n = n - earlier
            if t is not None or n > 0:
                eng.wait_ge(self.done[bank], n)


def retention_moe(nc, x, small, layer_w, w1, w3, w2, b2, out):
    where, n_small = columns(SMALL)
    where_w, n_layer = columns(LAYER_W)
    x_v = x.rearrange("a (m i p) d -> (a m) p i d", i=NT, p=P)
    out_v = out.rearrange("a (m i p) d -> (a m) p i d", i=NT, p=P)

    with ExitStack() as ctx:
        def sb(name, shape, dtype=F32):
            return ctx.enter_context(nc.sbuf_tensor(name, shape, dtype))

        def psum(name, shape):
            return ctx.enter_context(nc.psum_tensor(name, shape, F32))

        def sem(name):
            return ctx.enter_context(nc.semaphore(name))

        small_s = sb("small_s", [P, n_small])
        layer_s = sb("layer_s", [P, LAYERS, n_layer])
        up_hi = sb("up_hi", [P, 2, UNITS, KB * P], F32R)
        up_lo = sb("up_lo", [P, 2, UNITS, KB * P], F32R)
        layer_hi = sb("layer_hi", [P, LAYERS, (1 + FFN) * P], F32R)
        layer_lo = sb("layer_lo", [P, LAYERS, (1 + FFN) * P], F32R)
        w2_s = sb("w2_s", [P, UNITS, KB, P])
        b2_s = sb("b2_s", [EXPERTS, P])
        minus_half = sb("minus_half", [P, NT])
        out_bias = sb("out_bias", [P, P])
        pool_carrier = sb("pool_carrier", [P, 3 * len(STEPS)])
        dve_carrier = sb("dve_carrier", [P, len(STEPS)])

        x_in = sb("x_in", [P, NT, P])
        xn_next = sb("xn_next", [P, NT, P])
        xnT_next = sb("xnT_next", [P, MT])
        cw_next = sb("cw_next", [P, NT, EXPERTS])
        cwT_next = sb("cwT_next", [EXPERTS, MT])
        acc_next = sb("acc_next", [P, NT, P])
        stats_next = sb("stats_next", [P, NT, 6])
        mean_var_next = sb("mean_var_next", [P, NT, 2])
        var_eps_next = sb("var_eps_next", [P, NT])
        rstd_next = sb("rstd_next", [P, NT])
        logits = sb("logits", [P, NT, EXPERTS])
        top = sb("top", [P, NT])
        shifted = sb("shifted", [P, NT, EXPERTS])
        exps = sb("exps", [P, NT, EXPERTS])
        above = sb("above", [P, NT, EXPERTS, EXPERTS])
        ties = sb("ties", [P, NT, EXPERTS, EXPERTS])
        rank = sb("rank", [P, NT, EXPERTS])
        chosen = sb("chosen", [P, NT, EXPERTS])
        exps_sum = sb("exps_sum", [P, NT])
        chosen_sum = sb("chosen_sum", [P, NT])
        scale = sb("scale", [P, NT])

        res = sb("res", [P, NT, P])
        xnT_hi = sb("xnT_hi", [P, MT], F32R)
        xnT_lo = sb("xnT_lo", [P, MT], F32R)
        cw = sb("cw", [P, NT, EXPERTS])
        acc = sb("acc", [P, NT, P])
        stats = sb("stats", [P, NT, 6])
        mean_var = sb("mean_var", [P, NT, 2])
        var_eps = sb("var_eps", [P, NT])
        rstd = sb("rstd", [P, NT])
        normed = sb("normed", [P, NT, P])
        hT = sb("hT", [P, MT])
        hT_hi = sb("hT_hi", [P, MT], F32R)
        hT_lo = sb("hT_lo", [P, MT], F32R)
        qT = sb("qT", [P, NT, P])
        q_hi, q_lo, k_hi, k_lo = [sb(n, [P, MT], F32R) for n in ("q_hi", "q_lo", "k_hi", "k_lo")]
        select = sb("select", [P, 4, GROUPS, P], F32R)
        k_stack = sb("k_stack", [P, 2, MT], F32R)
        q_stack = sb("q_stack", [P, 2, NT, GH, P], F32R)
        kT = sb("kT", [P, NT, P])
        k_tok = sb("k_tok", [P, NT, P])
        v_tok = sb("v_tok", [P, NT, P])
        v_heads = sb("v_heads", [P, NT, GROUPS, GH * GP])
        gateT = sb("gateT", [P, MT])
        scores = sb("scores", [P, 4, GH, P])
        chunk_kv = sb("chunk_kv", [P, NT, P])
        state = sb("state", [P, LAYERS, NT, P])
        gelus = sb("gelus", [P, FFN, MT])
        silus = sb("silus", [P, 2, MT])
        hidden = sb("hidden", [P, 2, KB, MT])
        out_s = sb("out_s", [P, NT, P])

        shared_p = psum("shared_p", [P, 2, MT])
        scores_p = psum("scores_p", [P, 2, MT])
        ret_p = psum("ret_p", [P, MT])
        up_p = psum("up_p", [P, 2, MT])
        down_p = psum("down_p", [P, MT])

        def col(name, l=None):
            a, b = where[name if l is None else f"{name}_{l}"]
            return small_s[:, a:b]

        def over(ap, n=NT):
            return ap.unsqueeze(1).broadcast_to([P, n, ap.shape[-1]])

        def up_banks(step):
            return scores_p if step in BORROWING else up_p

        def up_part(parts, w, units):
            return parts[:, w, units].rearrange("p u c -> p (u c)")

        def layer_part(parts, name, l):
            return parts[:, l, 0:2 * P] if name == "qx" else parts[:, l, 2 * P:]

        def weight(name, l):
            a, b = where_w[name]
            return layer_s[:, l, a:b]

        def layer_piece(name, l, *when):
            whole = weight(name, l)[:, P:] if name == "ffn1" else weight(name, l)
            return whole, layer_part(layer_hi, name, l), layer_part(layer_lo, name, l), *when

        def up_piece(w, first, n, landed, *when):
            units = slice(first, first + n)
            return landed, up_part(up_hi, w, units), up_part(up_lo, w, units), *when

        half, rest = EXPERTS // 2, UNITS - EXPERTS
        hidden_flat, gelus_flat = hidden[:].rearrange("p a k n -> p (a k n)"), gelus[:].rearrange("p a n -> p (a n)")
        width = half * KB * P
        pieces = {
            "qx_0": layer_piece("qx", 0, ("load",), "dve", ("next_norm",)),
            "w1_0": up_piece(0, 0, half, hidden_flat[:, 0:width], ("next_turn",), "dve", ("turn", 0, 1)),
            "w3_0": up_piece(1, 0, half, hidden_flat[:, width:], ("next_turn",), "dve", ("turn", 0, 1)),
            "w1_4": up_piece(0, half, half, gelus_flat[:, 0:width], ("turn", 0, 1), "pool", ("turn", 0, 1)),
            "w3_4": up_piece(1, half, half, gelus_flat[:, width:], ("turn", 0, 1), "pool", ("turn", 0, 1)),
            "w1_8": up_piece(0, EXPERTS, rest, chunk_kv[:].rearrange("p i n -> p (i n)"), ("turn", 0, 1), "pool", ("turn", 0, 1)),
            "w3_8": up_piece(1, EXPERTS, rest, out_s[:].rearrange("p i n -> p (i n)"), ("turn", 0, 1), "pool", ("turn", 0, 1)),
            "ffn1_0": layer_piece("ffn1", 0, ("next_acc",), "pool", ("next_acc",)),
            "qx_1": layer_piece("qx", 1, ("next_acc",), "pool", ("next_acc",)),
            "ffn1_1": layer_piece("ffn1", 1, ("next_acc",), "pool", ("next_acc",))}

        def upper_parts(act, step):
            for name, (landed, hi, _, when, _, _) in pieces.items():
                if when == step:
                    act.wait_ge(s_piece[name], 16)
                    act.activation(hi, landed, ACT.Copy).then_inc(s_hi[name], 1)

        def lower_parts(eng, me, step):
            for name, (landed, hi, lo, _, by, when) in pieces.items():
                if (by, when) == (me, step):
                    eng.wait_ge(s_hi[name], 1)
                    eng.tensor_tensor(lo, landed, hi.bitcast(F32), ALU.subtract).then_inc(s_lo[name], 1)

        def tiles(ap):
            return ap.rearrange("p (i n) -> p i n", i=NT)

        def tile_of(ap, i):
            return ap[:, i * P:(i + 1) * P]

        s_small, s_reto_ffn2, s_w2, s_b2 = [sem(f"{n}_loaded") for n in ("small", "reto_ffn2", "w2", "b2")]
        s_k, s_v = [[sem(f"{n}_{l}_loaded") for l in range(LAYERS)] for n in ("k", "v")]
        s_piece, s_hi, s_lo = [{name: sem(f"{name}_{what}") for name in pieces} for what in ("loaded", "hi_ready", "lo_ready")]
        s_x = sem("x_loaded")
        s_select_zero = sem("select_zero")
        s_select = sem("select_ready")
        s_filled = sem("constants_filled")
        s_out_bias = sem("out_bias_ready")
        s_stored = sem("out_stored")

        x_biased_ready = Count(sem("x_biased_ready"), {"next_norm": 1})
        var_next_ready = Count(sem("var_next_ready"), {"next_norm": 1})
        rstd_next_ready = Count(sem("rstd_next_ready"), {"next_norm": 1})
        xn_next_ready = Count(sem("xn_next_ready"), {"next_norm": 1})
        shifted_ready = Count(sem("shifted_ready"), {"next_gate": 1})
        exps_ready = Count(sem("exps_ready"), {"next_gate": 1})
        cw_next_ready = Count(sem("cw_next_ready"), {"next_choose": 1})
        begun = Count(sem("begin_copies"), {"begin": 2})
        xnT_ready = Count(sem("xnT_ready"), {"next_parts": 1})
        var_ready = Count(sem("var_ready"), {"norm": 1})
        rstd_ready = Count(sem("rstd_ready"), {"norm": 1})
        normed_ready = Count(sem("normed_ready"), {"apply": 1})
        res_biased = Count(sem("res_biased"), {"apply": 1, ("apply", 0, 1): 0})
        h_hi_ready = Count(sem("hT_hi_ready"), {"turn": 1})
        h_lo_ready = Count(sem("hT_lo_ready"), {"turn": 1})
        hi_ready = Count(sem("k_and_q_hi_ready"), {"project": 2})
        k_lo_ready = Count(sem("k_lo_ready"), {"project": 1})
        q_lo_ready = Count(sem("q_lo_ready"), {"project": 1})
        xn_lo_ready = Count(sem("xn_lo_ready"), {"next_parts": 1})
        v_heads_ready = Count(sem("v_heads_ready"), {"project": 1})
        state_ready = Count(sem("state_ready"), {"state": NT - 1, "inter": 1}, credit=1)
        scored = Count(sem("scores_in_psum"), {"score": 2})
        masked = Count(sem("scores_masked"), {"score": 2})
        scores_used = Count(sem("scores_used"), {"pv": 2})
        retained = Count(sem("retention_in_psum"), {"inter": 1})
        gated = Count(sem("retention_gated"), {"inter": 1})
        w1_ready = Count(sem("w1_product"), {"moe": 1})
        w3_ready = Count(sem("w3_product"), {"moe": 1})
        silu_ready = Count(sem("silu_ready"), {"moe": 1}, credit=1)
        hidden_ready = Count(sem("hidden_ready"), {"moe": 1}, credit=2)
        down_ready = Count(sem("down_product"), {"down": 1}, credit=1)
        acc_updated = Count(sem("acc_updated"), {"down": 1}, credit=1)
        out_ready = Count(sem("out_ready"), {"finish": 1})
        dve_link = Count(sem("vector_link"), {"norm": 2, "next_norm": 2, "next_gate": 5, "next_choose": 4}, steps=DVE_STEPS)
        shared = SharedBanks(sem("shared_product"), [sem("shared_taken_0"), sem("shared_taken_1")])

        def run(eng, step_of, steps=STEPS, weights_parts=lambda step: None):
            start, body, last = phases(steps)
            for step in start:
                step_of(None, step)
                weights_parts(step)
            with eng.Fori(0, MACROS - 1) as t:
                for step in body:
                    step_of(t, step)
            for step in last:
                step_of(MACROS - 1, step)

        block = ctx.enter_context(nc.Block())

        @block.sync
        def _(sp):
            sp.dma_start(x_in[:], x_v[0, :, :, :]).then_inc(s_x, 16)

            def load(name, source):
                sp.dma_start(pieces[name][0], source).then_inc(s_piece[name], 16)

            def load_layer(l, names, s_loaded):
                fields = slice(where_w[names[0]][0], where_w[names[-1]][1])
                sp.dma_start(layer_s[:, l, fields], layer_w[:, l, fields]).then_inc(s_loaded, 16)

            load_layer(0, ["k"], s_k[0])
            load_layer(0, ["qx"], s_piece["qx_0"])
            load_layer(0, ["v"], s_v[0])
            for first, n in ((0, half), (half, half), (EXPERTS, rest)):
                for name, w in (("w1", w1), ("w3", w3)):
                    load(f"{name}_{first}", w[:, first:first + n, :].rearrange("p u c -> p (u c)"))
            load_layer(0, ["ffn1"], s_piece["ffn1_0"])
            load_layer(0, ["reto", "ffn2"], s_reto_ffn2)
            load_layer(1, ["k"], s_k[1])
            load_layer(1, ["qx"], s_piece["qx_1"])
            load_layer(1, ["v"], s_v[1])
            load_layer(1, ["ffn1"], s_piece["ffn1_1"])
            load_layer(1, ["reto", "ffn2"], s_reto_ffn2)
            sp.dma_start(w2_s[:], w2).then_inc(s_w2, 16)

            def step_of(t, step):
                if step[0] == "load" and t is not None:
                    xn_next_ready.wait_all_before(sp, t, step)
                    x_biased_ready.wait_all_before(sp, t, step)
                    sp.dma_start(x_in[:], x_v[t + 1, :, :, :]).then_inc(s_x, 16)
                if step[0] == "finish":
                    out_ready.wait(sp, t, step, 1)
                    sp.dma_start(out_v[t, :, :, :], out_s[:]).then_inc(s_stored, 16)

            run(sp, step_of)
            sp.wait_ge(s_stored, 16 * (MACROS + 1))

        @block.gpsimd
        def _(pool):
            pool.memset(minus_half[:], -0.5).then_inc(s_filled, 1)
            pool.memset(state[:], 0.0).then_inc(state_ready.sem, 1)
            pool.memset(v_heads[:], 0.0).then_inc(s_filled, 1)
            pool.wait_ge(s_filled, 2)

            def carry_wait(step, n=0):
                c = 3 * STEPS.index(step) + n
                pool.tensor_tensor(pool_carrier[:, c:c + 1], minus_half[:, 0:1], minus_half[:, 0:1], ALU.mult)

            def inverse_std(var_eps, done, to):
                pool.tensor_tensor(to[:], var_eps[:], minus_half[:], ALU.pow).then_inc(done.sem, 1)

            def step_of(t, step):
                kind = step[0]
                if kind == "begin":
                    normed_ready.wait_all_before(pool, t, step)
                    pool.tensor_tensor(res[:], xn_next[:], over(col("reto_b", 0)), ALU.add).then_inc(begun.sem, 1)
                    acc_updated.wait_all_before(pool, t, step)
                    cw_next_ready.wait_all_before(pool, t, step)
                    carry_wait(step)
                    pool.tensor_copy(cw[:], cw_next[:]).then_inc(begun.sem, 1)
                elif kind == "next_norm":
                    var_next_ready.wait(pool, t, step, 1)
                    inverse_std(var_eps_next, rstd_next_ready, rstd_next)
                    if t is None:
                        pool.wait_ge(s_small, 16)
                        pool.tensor_tensor(out_bias[:], col("lnf_b"), col("sb2"), ALU.add).then_inc(s_out_bias, 1)
                        pool.wait_ge(s_out_bias, 1)
                    else:
                        acc_updated.wait(pool, t, ("down", 0), 1)
                    pool.wait_ge(s_x, 16 if t is None else t * 16 + 32)
                    pool.tensor_tensor(acc_next[:], x_in[:], over(out_bias[:]), ALU.add).then_inc(x_biased_ready.sem, 1)
                elif kind == "norm":
                    var_ready.wait(pool, t, step, 1)
                    inverse_std(var_eps, rstd_ready, rstd)
                elif kind == "apply":
                    l, w = step[1:]
                    normed_ready.wait(pool, t, step, 1)
                    if w == 3:
                        pool.tensor_tensor(out_s[:], out_s[:], over(col("lnf_g")), ALU.mult).then_inc(res_biased.sem, 1)
                    elif (l, w) != (0, 1):
                        bias = col("reto_b" if w == 1 else "ffn2_b", l)
                        pool.tensor_tensor(res[:], res[:], over(bias), ALU.add).then_inc(res_biased.sem, 1)
                elif kind == "project":
                    l = step[1]
                    hi_ready.wait(pool, t, step, 1)
                    pool.tensor_tensor(k_lo[:], kT[:].rearrange("p i n -> p (i n)"), k_hi[:].bitcast(F32),
                                       ALU.subtract).then_inc(k_lo_ready.sem, 1)
                    shared.wait_taken(pool, t, (step, 3))
                    carry_wait(step)
                    for i in range(NT):
                        own = v_heads[:, i].rearrange("p g (b e) -> p g b e", e=HD)[:, :, 0:GH * GH:GH + 1, :]
                        ins = pool.tensor_copy(own, v_tok[:, i].rearrange("p (g j e) -> p g j e", g=GROUPS, e=HD))
                    ins.then_inc(v_heads_ready.sem, 1)

            run(pool, step_of, weights_parts=lambda step: lower_parts(pool, "pool", step))

        @block.scalar
        def _(act):
            act.dma_start(small_s[:], small).then_inc(s_small, 16)
            act.dma_start(b2_s[:], b2).then_inc(s_b2, 16)
            act.wait_ge(s_small, 16)
            act.activation(silus[:, 0, 0:1], col("ident")[:, 0:1], ACT.Copy).then_inc(silu_ready.sem, 1)
            act.wait_ge(s_select_zero, 1)
            for part, copies in enumerate(((0, 2), (1, 3), (0, 1), (2, 3))):
                for c in copies:
                    act.activation(select[:, part, :, c * GP:(c + 1) * GP], col("ident").rearrange("p (g n) -> p g n", g=GROUPS),
                                   ACT.Copy).then_inc(s_select, 1)

            def take(t, step, j, to, func=ACT.Copy, **more):
                shared.wait_product(act, t, step, j)
                bank = shared.bank(t, step, j)
                return act.activation(to, shared_p[0:to.shape[0], bank, :], func, **more).then_inc(shared.done[bank], 1)

            def step_of(t, step):
                kind = step[0]
                if kind == "next_parts":
                    if t is not None:
                        w3_ready.wait(act, t, ("moe", UNITS - 1, KB - 1), 1)
                    act.activation(xnT_hi[:], xnT_next[:], ACT.Copy).then_inc(xnT_ready.sem, 1)
                elif kind == "next_turn":
                    if t is not None:
                        xnT_ready.wait_all_before(act, t, step)
                    take(t, step, 0, xnT_next[:])
                elif kind == "next_gate":
                    shifted_ready.wait(act, t, step, 1)
                    act.activation(exps[:], shifted[:], ACT.Exp).then_inc(exps_ready.sem, 1)
                elif kind == "next_bias":
                    take(t, step, 0, cwT_next[:])
                elif kind == "turn":
                    l, w = step[1:]
                    take(t, step, 0, hT[:], ACT.Identity, scale=col(f"ln{w}_g", l), bias=col(f"ln{w}_b", l))
                    shared.wait_taken(act, t, (step, 0))
                    act.activation(hT_hi[:], hT[:], ACT.Copy).then_inc(h_hi_ready.sem, 1)
                elif kind == "project":
                    for n, (whole, hi) in enumerate(((kT, k_hi), (qT, q_hi))):
                        shared.wait_taken(act, t, (step, n))
                        act.activation(hi[:], whole[:].rearrange("p i n -> p (i n)"), ACT.Copy).then_inc(hi_ready.sem, 1)
                    take(t, step, 2, gateT[:], ACT.Silu, bias=col("bx", step[1]))
                elif kind == "stack":
                    g = step[2]
                    take(t, step, 0, k_stack[:, g % 2, :])
                    shared.wait_product(act, t, step, 1)
                    for j in range(GH):
                        ins = act.activation(q_stack[:, g % 2, :, j, :], tiles(shared_p[:, shared.bank(t, step, 1), :]), ACT.Copy,
                                             scale=col("head_mask")[:, j:j + 1])
                    ins.then_inc(shared.done[shared.bank(t, step, 1)], 1)
                elif kind == "turn_k":
                    take(t, step, 0, k_tok[:].rearrange("p i n -> p (i n)"))
                elif kind == "ffn1":
                    for f in range(FFN):
                        take(t, step, f, gelus[:, f, :], ACT.Gelu, bias=col("ffn1_b", step[1])[:, f:f + 1])
                elif kind == "moe":
                    u, k = step[1:]
                    w1_ready.wait(act, t, step, 1)
                    hidden_ready.wait(act, t, step, -1)
                    act.activation(silus[:, k, :], up_banks(step)[:, 0, :], ACT.Silu,
                                   bias=col("b1")[:, u * KB + k:u * KB + k + 1]).then_inc(silu_ready.sem, 1)

            run(act, step_of, ACT_STEPS, lambda step: upper_parts(act, step))

        @block.vector
        def _(dve):
            dve.memset(stats[:], 0.0).then_inc(hidden_ready.sem, 2)
            dve.memset(mean_var[:], 0.0).then_inc(acc_updated.sem, 1)
            dve.memset(rank[:], 0.0).then_inc(s_stored, 16)
            dve.memset(exps_sum[:], 0.0).then_inc(shared.done[0], shared.skipped)
            dve.memset(select[:].bitcast(F32), 0.0).then_inc(s_select_zero, 1)
            linked = [None, 0]

            def link(t, step, ins):
                if linked[0] != (phase_of(t), step):
                    linked[:] = [(phase_of(t), step), 0]
                linked[1] += 1
                ins.then_inc(dve_link.sem, 1)
                dve_link.wait(dve, t, step, linked[1])

            def statistics(t, step, rows, stats, mean_var, var_eps, var_done):
                for i in range(NT):
                    ins = dve.bn_stats(stats[:, i, :], rows[:, i, :])
                link(t, step, ins)
                c = STEPS.index(step)
                dve.memset(dve_carrier[:, c:c + 1], 0.0)
                for i in range(NT):
                    ins = dve.bn_aggr(mean_var[:, i, :], stats[:, i, :])
                link(t, step, ins)
                dve.tensor_scalar(var_eps[:], mean_var[:, :, 1], EPS, None, ALU.add).then_inc(var_done.sem, 1)

            def normalise(rows, mean_var, rstd, to, done):
                for i in range(NT):
                    ins = dve.tensor_scalar(to[:, i, :], rows[:, i, :], mean_var[:, i, 0:1], rstd[:, i:i + 1],
                                            ALU.subtract, ALU.mult)
                ins.then_inc(done.sem, 1)

            def product(t, step, j=0):
                shared.wait_product(dve, t, step, j)
                return shared_p[:, shared.bank(t, step, j), :]

            def taken(t, step, j, ins):
                ins.then_inc(shared.done[shared.bank(t, step, j)], 1)

            def gate(t, step):
                p = product(t, step)[:, 0:NT * EXPERTS].rearrange("p (i e) -> p i e", e=EXPERTS)
                taken(t, step, 0, dve.tensor_tensor(logits[:], p, over(col("gate_b")), ALU.add))
                shared.wait_taken(dve, t, (step, 0))
                mine = logits[:].unsqueeze(3).broadcast_to([P, NT, EXPERTS, EXPERTS])
                other = logits[:].unsqueeze(2).broadcast_to([P, NT, EXPERTS, EXPERTS])
                link(t, step, dve.tensor_reduce(top[:], logits[:], AX_X, ALU.max))
                dve.tensor_tensor(shifted[:], logits[:], top[:].unsqueeze(2).broadcast_to([P, NT, EXPERTS]),
                                  ALU.subtract).then_inc(shifted_ready.sem, 1)
                dve.tensor_tensor(above[:], other, mine, ALU.is_gt)
                link(t, step, dve.tensor_tensor(ties[:], other, mine, ALU.is_equal))
                flat = "p i a b -> p i (a b)"
                link(t, step, dve.tensor_tensor(ties[:].rearrange(flat), ties[:].rearrange(flat), over(col("before")), ALU.mult))
                link(t, step, dve.tensor_tensor(above[:], above[:], ties[:], ALU.add))
                link(t, step, dve.tensor_reduce(rank[:], above[:], AX_X, ALU.add))

            def choose(t, step):
                exps_ready.wait(dve, t, ("next_gate",), 1)
                dve.tensor_reduce(exps_sum[:], exps[:], AX_X, ALU.add)
                link(t, step, dve.scalar_tensor_tensor(out=chosen[:], in0=rank[:], scalar=1.5, in1=exps[:],
                                                       op0=ALU.is_lt, op1=ALU.mult))
                link(t, step, dve.tensor_reduce(chosen_sum[:], chosen[:], AX_X, ALU.add))
                link(t, step, dve.scalar_tensor_tensor(out=chosen_sum[:], in0=exps_sum[:], scalar=1e-20, in1=chosen_sum[:],
                                                       op0=ALU.mult, op1=ALU.add))
                link(t, step, dve.reciprocal(scale[:], chosen_sum[:]))
                if t is not None:
                    begun.wait_all_before(dve, t, step)
                dve.tensor_tensor(cw_next[:], chosen[:], scale[:].unsqueeze(2).broadcast_to([P, NT, EXPERTS]),
                                  ALU.mult).then_inc(cw_next_ready.sem, 1)

            def add_to_acc(t, step, u):
                down_ready.wait(dve, t, step, 1)
                acc_updated.wait(dve, t, step, 0)
                sums = acc
                if u == 0:
                    begun.wait(dve, t, ("begin",), 2)
                    shared.wait_taken(dve, t, (("made", "next_acc"), 0))
                    sums = acc_next
                if u < EXPERTS:
                    for i in range(NT):
                        ins = dve.scalar_tensor_tensor(out=acc[:, i, :], in0=tile_of(down_p, i), scalar=cw[:, i, u:u + 1],
                                                       in1=sums[:, i, :], op0=ALU.mult, op1=ALU.add)
                else:
                    ins = dve.tensor_tensor(acc[:], tiles(down_p[:]), acc[:], ALU.add)
                ins.then_inc(acc_updated.sem, 1)

            def step_of(t, step):
                kind = step[0]
                if kind == "next_parts":
                    xnT_ready.wait(dve, t, step, 1)
                    dve.tensor_tensor(xnT_lo[:], xnT_next[:], xnT_hi[:].bitcast(F32), ALU.subtract).then_inc(xn_lo_ready.sem, 1)
                elif kind == "next_norm":
                    dve.wait_ge(s_x, 16 if t is None else t * 16 + 32)
                    if t is not None:
                        begun.wait(dve, t, ("begin",), 1)
                    statistics(t, step, x_in, stats_next, mean_var_next, var_eps_next, var_next_ready)
                    rstd_next_ready.wait(dve, t, step, 1)
                    normalise(x_in, mean_var_next, rstd_next, xn_next, xn_next_ready)
                elif kind == "next_gate":
                    gate(t, step)
                elif kind == "next_choose":
                    choose(t, step)
                elif kind == "next_acc":
                    x_biased_ready.wait(dve, t, ("next_norm",), 1)
                    taken(t, step, 0, dve.tensor_tensor(acc_next[:], tiles(product(t, step)), acc_next[:], ALU.add))
                elif kind == "norm":
                    l, w = step[1:]
                    if (l, w) == (0, 1):
                        xn_next_ready.wait(dve, t, ("next_norm",), 1)
                    else:
                        shared.wait_taken(dve, t, (("reto", l) if w == 2 else ("ffn2", l - 1 if w == 1 else l), 0))
                    statistics(t, step, xn_next if (l, w) == (0, 1) else res, stats, mean_var, var_eps, var_ready)
                elif kind == "apply":
                    l, w = step[1:]
                    if (l, w) == (0, 1) and t is not None:
                        shared.wait_product(dve, t, ("turn", LAYERS - 1, 2))
                    if w == 3:
                        dve.wait_ge(s_stored, t * 16 + 16)
                    rstd_ready.wait(dve, t, ("norm", l, w), 1)
                    normalise(xn_next if (l, w) == (0, 1) else res, mean_var, rstd, out_s if w == 3 else normed, normed_ready)
                elif kind == "turn":
                    h_hi_ready.wait(dve, t, step, 1)
                    dve.tensor_tensor(hT_lo[:], hT[:], hT_hi[:].bitcast(F32), ALU.subtract).then_inc(h_lo_ready.sem, 1)
                elif kind == "project":
                    l = step[1]
                    for j, (to, bias, decay) in enumerate(((kT, "bk", "decay_k"), (qT, "bq", "decay_q"))):
                        taken(t, step, j, dve.scalar_tensor_tensor(out=to[:], in0=tiles(product(t, step, j)), scalar=col(bias, l),
                                                                   in1=over(col(decay)), op0=ALU.add, op1=ALU.mult))
                    hi_ready.wait(dve, t, step, 2)
                    dve.tensor_tensor(q_lo[:], qT[:].rearrange("p i n -> p (i n)"), q_hi[:].bitcast(F32),
                                      ALU.subtract).then_inc(q_lo_ready.sem, 1)
                    taken(t, step, 3, dve.tensor_tensor(v_tok[:], tiles(product(t, step, 3)), over(col("bv", l)), ALU.add))
                elif kind == "state":
                    l = step[1]
                    taken(t, step, 0, dve.scalar_tensor_tensor(out=chunk_kv[:], in0=tiles(product(t, step)), scalar=col("decay_chunk"),
                                                               in1=over(col("same_head")), op0=ALU.mult, op1=ALU.mult))
                    shared.wait_taken(dve, t, (step, 0))
                    for i in range(NT - 1):
                        state_ready.wait(dve, t, step, i)
                        next_state(l, i)
                elif kind == "score":
                    for n in range(2):
                        if step[2] > 0:
                            scores_used.wait(dve, t, ("pv", step[1], step[2] - 1, step[3]), n + 1)
                        scored.wait(dve, t, step, n + 1)
                        dve.tensor_tensor(scores[:, 2 * step[3] + n], scores_p[:, n, :].rearrange("p (j n) -> p j n", j=GH),
                                          over(col("causal"), GH), ALU.mult).then_inc(masked.sem, 1)
                elif kind == "inter":
                    l = step[1]
                    retained.wait(dve, t, step, 1)
                    shared.wait_taken(dve, t, (projected(l), 2))
                    dve.tensor_tensor(gateT[:], ret_p[:], gateT[:], ALU.mult).then_inc(gated.sem, 1)
                    state_ready.wait(dve, t, step, 0)
                    next_state(l, NT - 1)
                elif kind in ("reto", "ffn2"):
                    l = step[1]
                    if (kind, l) == ("reto", 0):
                        begun.wait(dve, t, ("begin",), 1)
                    else:
                        res_biased.wait(dve, t, ("apply", l, 1 if kind == "reto" else 2), 1)
                    taken(t, step, 0, dve.tensor_tensor(res[:], tiles(product(t, step)), res[:], ALU.add))
                elif kind == "moe":
                    u, k = step[1:]
                    silu_ready.wait(dve, t, step, 1)
                    w3_ready.wait(dve, t, step, 1)
                    b = u * KB + k
                    dve.scalar_tensor_tensor(out=hidden[:, u % 2, k, :], in0=up_banks(step)[:, 1, :], scalar=col("b3")[:, b:b + 1],
                                             in1=silus[:, k, :], op0=ALU.add, op1=ALU.mult).then_inc(hidden_ready.sem, 1)
                elif kind == "down":
                    add_to_acc(t, step, step[1])
                elif kind == "finish":
                    res_biased.wait(dve, t, ("apply", LAYERS - 1, 3), 1)
                    acc_updated.wait(dve, t, ("down", UNITS - 1), 1)
                    dve.tensor_tensor(out_s[:], out_s[:], acc[:], ALU.add).then_inc(out_ready.sem, 1)

            def next_state(l, i):
                dve.scalar_tensor_tensor(out=state[:, l, (i + 1) % NT], in0=state[:, l, i], scalar=col("decay_chunk"),
                                         in1=chunk_kv[:, i], op0=ALU.mult, op1=ALU.add).then_inc(state_ready.sem, 1)

            run(dve, step_of, DVE_STEPS, lambda step: lower_parts(dve, "dve", step))

        @block.tensor
        def _(pe):
            pe.wait_ge(s_small, 16)
            shared_ready = shared.ready.sem

            def use(t, step, j=0, of=()):
                shared.wait_taken(pe, t, *of, free=(step, j))
                return shared_p[:, shared.bank(t, step, j), :]

            def turn(to, rows):
                for i in range(NT):
                    ins = pe.transpose(tile_of(to, i)[0:rows.shape[2], :], rows[:, i, :], col("ident"))
                ins.then_inc(shared_ready, 1)

            def tokens_product(to, lhs, rhs):
                n = rhs[0].shape[-1]
                for i in range(NT):
                    for b, (left, right) in enumerate(zip(lhs, rhs)):
                        ins = pe.matmul(to[:, i * n:(i + 1) * n], tile_of(left, i), right,
                                        start=(b == 0), stop=(b == len(rhs) - 1))
                return ins

            def step_of(t, step):
                kind = step[0]
                if kind == "next_turn":
                    xn_next_ready.wait(pe, t, ("next_norm",), 1)
                    turn(use(t, step), xn_next)
                elif kind == "next_gate":
                    to = use(t, step, of=[(("next_turn",), 0)])
                    tokens_product(to, [xnT_next], [col("gate_w")]).then_inc(shared_ready, 1)
                elif kind == "next_bias":
                    cw_next_ready.wait(pe, t, ("next_choose",), 1)
                    turn(use(t, step), cw_next)
                elif kind == "next_acc":
                    to = use(t, step, of=[(("next_bias",), 0)])
                    pe.wait_ge(s_b2, 16)
                    tokens_product(to, [cwT_next], [b2_s[:]]).then_inc(shared_ready, 1)
                    if t is None:
                        pe.transpose(down_p[:, 0:P], col("ident"), col("ident")).then_inc(down_ready.sem, 1)
                elif kind == "turn":
                    normed_ready.wait(pe, t, ("apply", *step[1:]), 1)
                    turn(use(t, step), normed)
                elif kind == "project":
                    l = step[1]
                    pe.wait_ge(s_k[l], 16)
                    to = use(t, step, 0, of=[(("turn", l, 1), 0)])
                    pe.matmul(to, weight("k", l), hT[:], start=True, stop=True).then_inc(shared_ready, 1)
                    for j in (1, 2):
                        from_parts(t, step, j, "qx", j - 1, ("turn", l, 1))
                    pe.wait_ge(s_v[l], 16)
                    to = use(t, step, 3, of=[(("turn", l, 1), 0)])
                    tokens_product(to, [hT], [weight("v", l)]).then_inc(shared_ready, 1)
                elif kind == "stack":
                    l, g = step[1:]
                    pe.wait_ge(s_select, 8)
                    for j, (hi, lo) in enumerate(((k_hi, k_lo), (q_hi, q_lo))):
                        if g == 0:
                            (k_lo_ready, q_lo_ready)[j].wait(pe, t, projected(l), 1)
                        to = use(t, step, j)
                        pe.matmul(to, select[:, 2 * j, g], hi[:], start=True, stop=False)
                        pe.matmul(to, select[:, 2 * j + 1, g], lo[:], start=False, stop=True).then_inc(shared_ready, 1)
                elif kind == "turn_k":
                    turn(use(t, step, of=[(projected(step[1]), 0)]), kT)
                elif kind == "state":
                    l = step[1]
                    to = use(t, step, of=[(("turn_k", l), 0), (projected(l), 3)])
                    for i in range(NT):
                        ins = pe.matmul(tile_of(to, i), k_tok[:, i], v_tok[:, i], start=True, stop=True)
                    ins.then_inc(shared_ready, 1)
                elif kind == "score":
                    l, g, h = step[1:]
                    if h == 0:
                        shared.wait_taken(pe, t, (("stack", l, g), 0), (("stack", l, g), 1))
                    if (g, h) == (0, 0):
                        wait_half(t, hidden_ready, BANKS_BEFORE[step])
                    for n in range(2):
                        if (g, h) != (0, 0):
                            masked.wait(pe, t, ("score", l, *last_pair(g, h)), n + 1)
                        i = 2 * h + n
                        pe.matmul(scores_p[:, n, :], tile_of(k_stack[:, g % 2], i), q_stack[:, g % 2, i].rearrange("p j n -> p (j n)"),
                                  start=True, stop=True).then_inc(scored.sem, 1)
                elif kind == "pv":
                    l, g, h = step[1:]
                    if (g, h) == (0, 0):
                        v_heads_ready.wait(pe, t, projected(l), 1)
                    for n in range(2):
                        i = 2 * h + n
                        masked.wait(pe, t, ("score", *step[1:]), n + 1)
                        for j in range(GH):
                            ins = pe.matmul(ret_p[g * GP:(g + 1) * GP, i * P:(i + 1) * P], v_heads[:, i, g, j * GP:(j + 1) * GP],
                                            scores[:, i, j, :], start=(i == 0 and j == 0), stop=True, skip_group_check=True)
                        ins.then_inc(scores_used.sem, 1)
                elif kind == "inter":
                    l = step[1]
                    for i in range(NT):
                        if i < 2:
                            state_ready.wait(pe, t, ("state", l), i * (NT - 1))
                        ins = pe.matmul(tile_of(ret_p, i), state[:, l, i], qT[:, i], start=False, stop=True, skip_group_check=True)
                    ins.then_inc(retained.sem, 1)
                elif kind == "reto":
                    pe.wait_ge(s_reto_ffn2, 2 * 16)
                    gated.wait(pe, t, ("inter", step[1]), 1)
                    tokens_product(use(t, step), [gateT], [weight("reto", step[1])]).then_inc(shared_ready, 1)
                elif kind == "ffn1":
                    l = step[1]
                    if l == 0:
                        pe.wait_ge(s_piece["ffn1_0"], 16)
                    to = use(t, step, 0, of=[(("turn", l, 2), 0)])
                    pe.matmul(to, tile_of(weight("ffn1", l), 0), hT[:], start=True, stop=True).then_inc(shared_ready, 1)
                    for f in range(1, FFN):
                        from_parts(t, step, f, "ffn1", f - 1, ("turn", l, 2))
                elif kind == "ffn2":
                    l = step[1]
                    to = use(t, step, of=[(("ffn1", l), f) for f in range(FFN)])
                    tokens_product(to, [gelus[:, f, :] for f in range(FFN)],
                                   [tile_of(weight("ffn2", l), f) for f in range(FFN)]).then_inc(shared_ready, 1)
                elif kind == "moe":
                    u, k = step[1:]
                    if (u, k) == (0, 0):
                        xn_lo_ready.wait(pe, t, ("made", "next_parts"), 1)
                    if k == 0:
                        for name in ("w1", "w3"):
                            if f"{name}_{u}" in pieces:
                                pe.wait_ge(s_lo[f"{name}_{u}"], 1)
                    wait_half(t, silu_ready, BANKS_BEFORE[step])
                    up(up_banks(step), 0, u, k).then_inc(w1_ready.sem, 1)
                    wait_half(t, hidden_ready, BANKS_BEFORE[step])
                    up(up_banks(step), 1, u, k).then_inc(w3_ready.sem, 1)
                elif kind == "down":
                    down(t, step, step[1])

            def wait_half(t, count, half):
                count.wait(pe, t, half or ("moe", 0, 0), 1 if half else 0)

            def up(to, n, u, k):
                parts = ((up_hi, xnT_hi), (up_hi, xnT_lo), (up_lo, xnT_hi))
                for b, (w, xt) in enumerate(parts):
                    ins = pe.matmul(to[:, n, :], tile_of(w[:, n, u], k), xt[:], start=(b == 0), stop=(b == len(parts) - 1))
                return ins

            def from_parts(t, step, j, name, block_of, turned):
                l = step[1]
                pe.wait_ge(s_lo[f"{name}_{l}"], 1)
                to = use(t, step, j)
                h_hi_ready.wait(pe, t, turned, 1)
                hi, lo = [tile_of(layer_part(parts, name, l), block_of) for parts in (layer_hi, layer_lo)]
                pe.matmul(to, hi, hT_hi[:], start=True, stop=False)
                pe.matmul(to, lo, hT_hi[:], start=False, stop=False)
                h_lo_ready.wait(pe, t, turned, 1)
                pe.matmul(to, hi, hT_lo[:], start=False, stop=True).then_inc(shared_ready, 1)

            def down(t, step, u):
                if u == 0:
                    pe.wait_ge(s_w2, 16)
                hidden_ready.wait(pe, t, ("moe", u, KB - 1), 1)
                acc_updated.wait(pe, t, step, 0)
                tokens_product(down_p, [hidden[:, u % 2, k] for k in range(KB)],
                               [w2_s[:, u, k] for k in range(KB)]).then_inc(down_ready.sem, 1)

            run(pe, step_of)


IN_NAMES = ["L0_attn_x", "small", "layer_w", "w1", "w3", "w2", "b2"]


def decays():
    gamma = 1.0 - 2.0 ** (-5.0 - np.arange(HEADS))
    by_row = np.repeat(gamma, HD)[:, None]
    n = np.arange(P)[None, :]
    return (by_row ** n).astype(np.float32), (by_row ** -n).astype(np.float32), (by_row ** P).astype(np.float32)


def laid_out(a):
    a = {name: np.asarray(value) for name, value in a.items()}
    rows = lambda v: np.broadcast_to(v.reshape(1, -1), (P, v.size))
    cols = lambda v: v.reshape(-1, P).T
    decay_q, decay_k, decay_chunk = decays()
    r = np.arange(P)
    e = np.arange(EXPERTS)
    f = {
        "ident": np.eye(P, dtype=np.float32),
        "causal": (r[None, :] >= r[:, None]).astype(np.float32),
        "decay_q": decay_q, "decay_k": decay_k, "decay_chunk": decay_chunk,
        "same_head": (r[None, :] // HD == r[:, None] // HD).astype(np.float32),
        "head_mask": ((r[:, None] // HD) % GH == np.arange(GH)[None, :]).astype(np.float32),
        "before": rows((e[None, :] < e[:, None]).astype(np.float32)),
        "gate_b": rows(a["L0_ffn_gate_b"]), "gate_w": a["L0_ffn_gate_w"].T,
        "b1": np.concatenate([cols(a["L0_ffn_b1"]), cols(a["L0_ffn_sb1"])], 1),
        "b3": np.concatenate([cols(a["L0_ffn_b3"]), cols(a["L0_ffn_sb3"])], 1),
        "lnf_g": rows(a["L0_attn_lnf_g"]), "lnf_b": rows(a["L0_attn_lnf_b"]), "sb2": rows(a["L0_ffn_sb2"]),
    }
    for l in range(LAYERS):
        bq, bk, bv, bx = a["L0_attn_proj_b"][l].reshape(4, P)
        f |= {f"ln1_g_{l}": cols(a["L0_attn_ln1_g"][l]), f"ln1_b_{l}": cols(a["L0_attn_ln1_b"][l]),
              f"ln2_g_{l}": cols(a["L0_attn_ln2_g"][l]), f"ln2_b_{l}": cols(a["L0_attn_ln2_b"][l]),
              f"bq_{l}": cols(bq), f"bk_{l}": cols(bk), f"bx_{l}": cols(bx), f"bv_{l}": rows(bv),
              f"ffn1_b_{l}": cols(a["L0_attn_ffn1_b"][l]), f"reto_b_{l}": rows(a["L0_attn_reto_b"][l]),
              f"ffn2_b_{l}": rows(a["L0_attn_ffn2_b"][l])}
    small = np.concatenate([f[name] for name, _ in SMALL], 1)
    by_in = lambda w: w.reshape(LAYERS, -1, P, w.shape[-1]).transpose(2, 0, 1, 3).reshape(P, LAYERS, -1)
    wq, wk, wv, wx = np.split(a["L0_attn_proj_w"], 4, axis=-1)
    weights = {"k": wk, "qx": np.concatenate([wq, wx], -1), "v": wv} | {n: a[f"L0_attn_{n}_w"] for n in ("ffn1", "reto", "ffn2")}
    layer_w = np.concatenate([by_in(weights[n]) for n, _ in LAYER_W], 2)
    up = lambda w, sw: np.concatenate([w.transpose(2, 0, 1), sw.reshape(UNITS - EXPERTS, KB * P, P).transpose(2, 0, 1)], 1)
    w2, sw2 = a["L0_ffn_w2"], a["L0_ffn_sw2"]
    down = np.concatenate([w2.reshape(EXPERTS, P, KB, P).transpose(3, 0, 2, 1),
                           sw2.reshape(P, UNITS - EXPERTS, KB, P).transpose(3, 1, 2, 0)], 1)
    return {"L0_attn_x": a["L0_attn_x"], "small": small, "layer_w": layer_w, "w1": up(a["L0_ffn_w1"], a["L0_ffn_sw1"]),
            "w3": up(a["L0_ffn_w3"], a["L0_ffn_sw3"]), "w2": down, "b2": a["L0_ffn_b2"]}


def kernel(**inputs):
    import concourse.bacc as bacc
    from concourse.bass_utils import run_bass_kernel_spmd

    nc = bacc.Bacc("TRN2", target_bir_lowering=False, num_devices=1)
    arrays, args = {}, []
    placed = laid_out(inputs)
    for name in IN_NAMES:
        arrays[f"in_{name}"] = np.ascontiguousarray(placed[name])
        args.append(nc.dram_tensor(f"in_{name}", arrays[f"in_{name}"].shape, F32, kind="ExternalInput").ap())
    args.append(nc.dram_tensor("out", (1, N_TOK, P), F32, kind="ExternalOutput").ap())
    retention_moe(nc, *args)
    r = run_bass_kernel_spmd(nc, [arrays], core_ids=[0])
    return r.results[0]["out"]
```
